# Optimizing a Trainium2 kernel written in Bass

```python
import numpy as np
import jax
import jax.numpy as jnp

def _softmax(x, axis=-1):
    return jax.nn.softmax(x, axis=axis)

def _gelu(x):
    return jax.nn.gelu(x, approximate=True)

def _silu(x):
    return jax.nn.silu(x)

def _sigmoid(x):
    return jax.nn.sigmoid(x)

def _layernorm(x, axis=-1, eps=1e-05):
    m = jnp.mean(x, axis=axis, keepdims=True)
    v = jnp.var(x, axis=axis, keepdims=True)
    return (x - m) / jnp.sqrt(v + eps)

def _scatter_add(tgt, idx, src, axis=0):
    return tgt.at[idx].add(src)

def _segment_sum(src, seg, n):
    return jax.ops.segment_sum(src, seg, n)
kernel_name = 'mk_seq_postln_d1_jaxref_r8_22b9d2'

def setup_inputs(seed: int=0):
    np.random.seed(seed)
    _w = jnp.asarray

    def _L0_attn_setup():
        import jax, jax.numpy as jnp
        import numpy as np
        B, S, E, H = (8, 128, 128, 16)
        EPS = 0.001
        key = jax.random.key(seed)
        ks = jax.random.split(key, 5)
        x = jax.random.normal(ks[0], (B, S, E), dtype=jnp.float32)
        Wq = jax.random.normal(ks[1], (E, E), dtype=jnp.float32) * 0.02
        Wk = jax.random.normal(ks[2], (E, E), dtype=jnp.float32) * 0.02
        Wv = jax.random.normal(ks[3], (E, E), dtype=jnp.float32) * 0.02
        rel_table = jax.random.normal(ks[4], (2 * S - 1, H), dtype=jnp.float32) * 0.02
        gamma = jnp.ones((E,), dtype=jnp.float32)
        beta = jnp.zeros((E,), dtype=jnp.float32)
        return {'x': x, 'Wq': Wq, 'Wk': Wk, 'Wv': Wv, 'rel_table': rel_table, 'gamma': gamma, 'beta': beta}
    _L0_attn_in = _L0_attn_setup()

    def _L0_ffn_setup():
        import jax, jax.numpy as jnp
        import numpy as np
        TOP_K = 4
        key = jax.random.key(seed)
        ks = jax.random.split(key, 5)
        B, T, D = (2, 128, 128)
        P, PD = (32, 32)
        return {'x': jax.random.normal(ks[0], (B, T, D), dtype=jnp.float32), 'hasher_w': jax.random.normal(ks[1], (PD, D), dtype=jnp.float32) * 0.03, 'keys': jax.random.normal(ks[2], (P, PD), dtype=jnp.float32) * 0.1, 'values_down': jax.random.normal(ks[3], (P, D, PD), dtype=jnp.float32) * 0.01, 'values_up': jax.random.normal(ks[4], (P, PD, D), dtype=jnp.float32) * 0.01, 'scale': jnp.full((1,), 0.1, dtype=jnp.float32)}
    _L0_ffn_in = _L0_ffn_setup()
    _d = {'L0_attn_x': _L0_attn_in['x'], 'L0_attn_Wq': _L0_attn_in['Wq'], 'L0_attn_Wk': _L0_attn_in['Wk'], 'L0_attn_Wv': _L0_attn_in['Wv'], 'L0_attn_rel_table': _L0_attn_in['rel_table'], 'L0_attn_gamma': _L0_attn_in['gamma'], 'L0_attn_beta': _L0_attn_in['beta'], 'L0_ffn_hasher_w': _L0_ffn_in['hasher_w'], 'L0_ffn_keys': _L0_ffn_in['keys'], 'L0_ffn_values_down': _L0_ffn_in['values_down'], 'L0_ffn_values_up': _L0_ffn_in['values_up'], 'L0_ffn_scale': _L0_ffn_in['scale']}
    _x0 = _d['L0_attn_x']
    _d['L0_attn_x'] = jax.random.normal(jax.random.fold_in(jax.random.key(seed), 1), (4, 512, 128), dtype=_x0.dtype)
    del _x0
    return _d

def reference(L0_attn_x, L0_attn_Wq, L0_attn_Wk, L0_attn_Wv, L0_attn_rel_table, L0_attn_gamma, L0_attn_beta, L0_ffn_hasher_w, L0_ffn_keys, L0_ffn_values_down, L0_ffn_values_up, L0_ffn_scale):

    def _L0_attn_ref(x, Wq, Wk, Wv, rel_table, gamma, beta):
        import jax, jax.numpy as jnp
        import numpy as np
        B, S, E, H = (8, 128, 128, 16)
        EPS = 0.001
        b, s, e = x.shape
        h = rel_table.shape[1]
        scale = e ** (-0.5)

        def split_heads(t):
            return t.reshape(b, s, h, -1).transpose(0, 2, 1, 3)
        q = split_heads(x @ Wq)
        k = split_heads(x @ Wk)
        v = split_heads(x @ Wv)
        attn = jnp.einsum('bhqd,bhkd->bhqk', q, k) * scale
        attn = jax.nn.softmax(attn, axis=-1)
        r = jnp.arange(s)
        rel_index = jnp.clip(r[None, :] - r[:, None] + (s - 1), 0, 2 * s - 2)
        bias = rel_table[rel_index]
        bias = bias.reshape(-1).reshape(h, s, s)
        attn = attn + bias[None]
        out = jnp.einsum('bhqk,bhkd->bhqd', attn, v)
        out = out.transpose(0, 2, 1, 3).reshape(b, s, e)
        mu = jnp.mean(out, axis=-1, keepdims=True)
        var = jnp.var(out, axis=-1, keepdims=True)
        out = (out - mu) / jnp.sqrt(var + EPS) * gamma + beta
        return out

    def _L0_ffn_ref(x, hasher_w, keys, values_down, values_up, scale):
        import jax, jax.numpy as jnp
        import numpy as np
        TOP_K = 4
        h = jnp.einsum('btd,pd->btp', x, hasher_w)
        sim = jnp.einsum('btp,np->btn', h, keys)
        vals, idx = jax.lax.top_k(sim, TOP_K)
        w = jax.nn.softmax(vals, axis=-1)
        out = jnp.zeros_like(x)
        for k in range(TOP_K):
            ik = idx[..., k]
            vd = values_down[ik]
            vu = values_up[ik]
            proj = jax.nn.silu(jnp.einsum('btd,btdp->btp', x, vd))
            o = jnp.einsum('btp,btpd->btd', proj, vu)
            out = out + o * w[..., k:k + 1]
        return x + out * scale
    x = L0_attn_x
    x = _layernorm(x + _L0_attn_ref(x, L0_attn_Wq, L0_attn_Wk, L0_attn_Wv, L0_attn_rel_table, L0_attn_gamma, L0_attn_beta), axis=-1)
    x = _layernorm(x + _L0_ffn_ref(x, L0_ffn_hasher_w, L0_ffn_keys, L0_ffn_values_down, L0_ffn_values_up, L0_ffn_scale), axis=-1)
    return x

_drawn_inputs = setup_inputs


def setup_inputs(seed=0):
    import zlib

    import numpy as np

    out = dict(_drawn_inputs(seed))
    spreads = {'L0_attn_gamma': (1.0, 0.2), 'L0_attn_beta': (0.0, 0.1)}
    factors = {'L0_attn_Wq': 8.0,
     'L0_attn_Wk': 8.0,
     'L0_ffn_hasher_w': 42.005,
     'L0_ffn_keys': 41.407,
     'L0_ffn_values_down': 44.173,
     'L0_ffn_values_up': 40.714}
    for name, (base, spread) in spreads.items():
        noise = np.random.default_rng([zlib.crc32(name.encode()), seed]).standard_normal(out[name].shape)
        drawn = base * np.exp(spread * noise) if base else spread * noise
        out[name] = jnp.asarray(drawn.astype(out[name].dtype))
    for name, factor in factors.items():
        out[name] = (out[name] * factor).astype(out[name].dtype)
    return out
```

```python
import concourse.bass as bass
from concourse import mybir
from contextlib import ExitStack


def bass_postln_attention_product_key_ffn(nc, x, w_q, w_k, w_v, rel_table, gamma, beta,
                                          hasher_w, keys, values_down, values_up, ffn_scale, out):
    F32, BF16 = mybir.dt.float32, mybir.dt.bfloat16
    ALU, ACT, AX = mybir.AluOpType, mybir.ActivationFunctionType, mybir.AxisListType

    B, S, E = x.shape
    H = rel_table.shape[1]
    D = E // H
    P = 128
    C = S // P
    J = 4
    G = H // J
    U = G * C
    NE, PD = keys.shape
    NJ = P // PD
    FJ = NE // NJ
    TOPK = 4
    PARTS = 3
    TERMS = PARTS * PARTS * D
    SHIFT_ROW = 96
    SCORE_SCALE = float(E) ** -0.5
    LEAD = 6
    HPB = S // H
    LAST = rel_table.shape[0] - 1
    NWIN = S
    TILE = 32
    EPS_ATTENTION, EPS_LN = 1e-3, 1e-5

    def constant_from(h):
        return min(max(-(-(LAST - S + HPB + HPB * h) // HPB), 0), H)

    CG = sum(constant_from((g + 1) * J - 1) == 0 for g in range(G))
    assert all(S - 1 - HPB * g * J + (C - 1) * P // H + HPB * constant_from((g + 1) * J - 1) < NWIN
               for g in range(CG, G)) and NWIN - P >= LAST and constant_from(H - 1) < H

    ctx = ExitStack()
    with ctx:
        def sb(name, shape, dt=F32):
            return ctx.enter_context(nc.sbuf_tensor(name, shape, dt))

        def pb(name, shape, dt=F32):
            return ctx.enter_context(nc.psum_tensor(name, shape, dt))

        def sem(name):
            return ctx.enter_context(nc.semaphore(name))

        ident, ident_bf = sb("ident", [P, P]), sb("ident_bf", [P, P], BF16)
        minus_half, zeros = sb("minus_half", [P, C]), sb("zeros", [P, NE])
        wq_sb, wk_sb, wv_sb = sb("wq_sb", [P, E]), sb("wk_sb", [P, E]), sb("wv_sb", [P, E])
        gamma_sb, beta_sb = sb("gamma_sb", [P, E]), sb("beta_sb", [P, E])
        hasher_sb, keys_sb, keys_t = sb("hasher_sb", [PD, E]), sb("keys_sb", [NE, PD]), sb("keys_t", [PD, NE])
        sim_w = sb("sim_w", [P, NE])
        down_sb = sb("down_sb", [P, NE, PD])
        up_sb = sb("up_sb", [P, FJ, E])
        scale_sb, half_scale = sb("scale_sb", [P, 1]), sb("half_scale", [P, 1])
        rel_win = sb("rel_win", [P, NWIN // P, P])
        rel_t = sb("rel_t", [P, NWIN])
        x_sb = sb("x_sb", [P, B, C, E])
        x_t = sb("x_t", [P, 2, S])
        parts = sb("parts", [P, 2, 2, PARTS, S], BF16)
        resid = sb("resid", [P, 2, S])
        v_all = sb("v_all", [P, C, H, B, D])
        v_cur = sb("v_cur", [P, C, H, TILE])
        q_stack, k_stack = sb("q_stack", [P, H, S], BF16), sb("k_stack", [P, H, S], BF16)
        neg_max = sb("neg_max", [P, 2, J * C])
        shift_parts = sb("shift_parts", [P, P // (J * C), J * C], BF16)
        shift_res = sb("shift_res", [P, J * C])
        shift_rows = sb("shift_rows", [PARTS * J * C, P], BF16)
        probs = sb("probs", [P, 2, J, S])
        o_sb = sb("o_sb", [P, S])
        rsum = sb("rsum", [P, C, J])
        attn = sb("attn", [P, C, E])
        bias_t = sb("bias_t", [P, 2, S])
        bias_v = sb("bias_v", [P, C, H, B, D])
        z = sb("z", [P, C, E])
        stats, mv = sb("stats", [P, C, 6]), sb("mv", [P, C, 2])
        veps, rstd = sb("veps", [P, C]), sb("rstd", [P, C])
        x1, x1_t = sb("x1", [P, C, E]), sb("x1_t", [P, S])
        sim, top = sb("sim", [P, C, NE]), sb("top", [P, C, 8])
        sdiff, sexp = sb("sdiff", [P, C, NE]), sb("sexp", [P, C, NE])
        above, ties, rank = sb("above", [P, C, NE]), sb("ties", [P, C, NE]), sb("rank", [P, C, NE])
        keep, mask, wexp = sb("keep", [P, C, NE]), sb("mask", [P, C, NE]), sb("wexp", [P, C, NE])
        n_above, wsum, winv, wscale = sb("n_above", [P, C]), sb("wsum", [P, C]), sb("winv", [P, C]), sb("wscale", [P, C])
        w_tok, w_t = sb("w_tok", [P, C, NE]), sb("w_t", [P, P])
        w_rows = sb("w_rows", [P, FJ, S])
        tanh_sb = sb("tanh_sb", [P, 2, S])
        hid = sb("hid", [P, FJ, S])
        y, y_out = sb("y", [P, C, E]), sb("y_out", [P, C, E])

        st_ps = pb("st_ps", [P, 2, 2, S])
        sm_ps = pb("sm_ps", [P, 2, S])
        ov_ps = pb("ov_ps", [P, S])
        mi_ps = pb("mi_ps", [P, S])

        stack_dram = nc.dram_tensor("stack_dram", [B, 2, H, D * PARTS * PARTS, S], BF16, kind="Internal").ap()
        rel_dram = nc.dram_tensor("rel_dram", [NWIN + P // H, H], F32, kind="Internal").ap()
        w_dram = nc.dram_tensor("w_dram", [NE, C, P], F32, kind="Internal").ap()

        waits_met = sem("waits_met")
        consts_made, stack_set = sem("consts_made"), sem("stack_set")
        x_loaded = [sem(f"x_loaded{b}") for b in range(B)]
        proj_loaded, rows_loaded = sem("proj_loaded"), sem("rows_loaded")
        rel_written, rel_loaded = sem("rel_written"), sem("rel_loaded")
        keys_loaded, experts_loaded = sem("keys_loaded"), sem("experts_loaded")
        prep_mm, prep_copied, prep_split = sem("prep_mm"), sem("prep_copied"), sem("prep_split")
        parts_written = [sem(f"parts_written{b}") for b in range(B)]
        stack_loaded = [sem(f"stack_loaded{g}") for g in range(G)]
        shift_loaded = [sem(f"shift_loaded{g}") for g in range(G)]
        table_mm, table_copied = sem("table_mm"), sem("table_copied")
        bias_mm, bias_copied, bias_turned, bias_kept = (
            sem("bias_mm"), sem("bias_copied"), sem("bias_turned"), sem("bias_kept"))
        scores_ready, probs_ready, pv_done = sem("scores_ready"), sem("probs_ready"), sem("pv_done")
        sm_ready, max_ready = sem("sm_ready"), sem("max_ready")
        shift_chain, shift_split = sem("shift_chain"), sem("shift_split")
        v_ready, o_copied, rsum_ready = sem("v_ready"), sem("o_copied"), sem("rsum_ready")
        xb_ready = sem("xb_ready")
        misc_ready, misc_done = sem("misc_ready"), sem("misc_done")
        dve_step, pool_step, act_step = sem("dve_step"), sem("pool_step"), sem("act_step")
        w_loaded = [sem(f"w_loaded{j}") for j in range(FJ)]
        w_written, y_stored = sem("w_written"), sem("y_stored")

        JOBS = {1: (["o3"], []), 2: (["shift1"], []), 5: (["o0", "x1t"], ["sim"]), 6: (["shift2"], ["down0"]),
                7: ([], ["down1"]), 8: ([], ["down2"]), 9: (["o1", "wt"], ["down3"]), 10: (["shift3"], ["down4"]),
                11: ([], ["down5"]), 12: ([], ["down6"]), 13: (["o2"], ["down7"]), 14: (["shift0"], ["up"])}
        OWN = ("shift0", "shift1", "shift2", "shift3", "o0", "o1", "o2")

        def jobs_of(attention, experts, more):
            def here(n):
                return (attention if n in OWN else experts) and (more or n != "shift0")
            return [n for u in sorted(JOBS) for half in JOBS[u] for n in half if here(n)]

        JOBS_FIRST, JOBS_EVERY = jobs_of(True, False, True), jobs_of(True, True, True)
        JOBS_LAST, JOBS_TAIL = jobs_of(True, True, False), jobs_of(False, True, False)

        def job(t, name):
            prologue = 1
            if isinstance(t, int) and t == 0:
                return prologue + JOBS_FIRST.index(name) + 1
            if isinstance(t, int) and t == B:
                return prologue + len(JOBS_FIRST) + (B - 2) * len(JOBS_EVERY) + len(JOBS_LAST) + JOBS_TAIL.index(name) + 1
            names = JOBS_LAST if isinstance(t, int) and t == B - 1 else JOBS_EVERY
            return (t - 1) * len(JOBS_EVERY) + (prologue + len(JOBS_FIRST) + names.index(name) + 1)

        def shift_job(t, g):
            return 1 if isinstance(t, int) and t == 0 and g == 0 else job(t - 1, "shift0") if g == 0 else job(t, f"shift{g}")

        def norm(k):
            return [k + "stats", k + "mv", k + "norm"]

        DVE_STEPS = (norm("a") + ["resid"] + norm("b") + ["top", "above", "ties", "n_above", "rank", "keep", "mask"]
                     + ["wexp", "wsum", "winv", "wscale", "w"] + norm("c"))
        POOL_STEPS = (["bias", "aeps", "apow", "gamma", "beps", "bpow", "sdiff"]
                      + [f"weigh{j}" for j in range(FJ)] + ["ceps", "cpow"])
        ACT_STEPS = ["sexp"] + [f"tanh{j}" for j in range(FJ)]

        def dve_at(f, name):
            return f * len(DVE_STEPS) + (DVE_STEPS.index(name) + 1)

        def pool_at(f, name):
            return f * len(POOL_STEPS) + (POOL_STEPS.index(name) + 1)

        def act_at(f, name):
            return f * len(ACT_STEPS) + (ACT_STEPS.index(name) + 1)

        def is0(t):
            return isinstance(t, int) and t == 0

        def apart(engine):
            engine.sem_inc(waits_met, 1)

        def rounds(engine, round_):
            round_(0, True, False, True)
            with engine.Fori(1, B - 1) as t:
                round_(t, True, True, True)
            round_(B - 1, True, True, False)
            round_(B, False, True, False)

        block = ctx.enter_context(nc.Block())

        @block.sync
        def _(sp):
            def load_slice(t, g):
                if not is0(t):
                    sp.wait_ge(scores_ready, (t - 1) * (2 * U) + 2 * C * (g + 1))
                    apart(sp)
                for a, stack in enumerate((q_stack, k_stack)):
                    src = stack_dram[t, a, g * J:(g + 1) * J]
                    sp.dma_start(stack[0:TERMS, g * J:(g + 1) * J, :], src.rearrange("h r s -> r h s")) \
                      .then_inc(stack_loaded[g], 16)

            def load_shift(t, g):
                sp.wait_ge(misc_done, shift_job(t, g))
                sp.dma_start(q_stack[SHIFT_ROW:SHIFT_ROW + PARTS, g * J:(g + 1) * J, :]
                             .rearrange("i h (c q) -> i (h c) q", c=C), shift_rows[:, :]).then_inc(shift_loaded[g], 16)

            sp.sem_inc(y_stored, 1)
            for b in range(B):
                sp.dma_start(x_sb[:, b], x[b].rearrange("(c p) e -> p c e", p=P)).then_inc(x_loaded[b], 16)
            sp.dma_start(rel_dram[0:LAST + 1, :], rel_table).then_inc(rel_written, 16)
            sp.dma_start(rel_dram[LAST + 1:, :],
                         bass.AP(rel_table.tensor, LAST * H, [[0, NWIN + P // H - LAST - 1], [1, H]])).then_inc(rel_written, 16)
            sp.wait_ge(rel_written, 32)
            sp.dma_start(rel_win[:], bass.AP(rel_dram.tensor, 0, [[H, P], [H * P, NWIN // P], [1, P]])) \
              .then_inc(rel_loaded, 16)
            for b in range(B):
                for a in range(2):
                    sp.wait_ge(prep_split, 3 * (2 * b + a) + 3)
                    rows = stack_dram[b, a].rearrange("h (d i j) s -> (h d) i j s", i=PARTS, j=PARTS)
                    for n in range(PARTS):
                        dst = rows[:, :, n, :] if a == 0 else rows[:, n, :, :]
                        sp.dma_start(dst, parts[:, b % 2, a]).then_inc(parts_written[b], 16)
                if b == 0:
                    sp.wait_ge(parts_written[0], 2 * PARTS * 16)
                    sp.wait_ge(stack_set, 2)
                    for g in range(G):
                        load_slice(0, g)
            for b in range(1, B):
                sp.wait_ge(parts_written[b], 2 * PARTS * 16)
            load_shift(0, 0)

            def round_(t, attention, experts, more):
                if attention:
                    if not is0(t):
                        load_slice(t, G - 1)
                    load_shift(t, 1)
                    if more:
                        load_slice(t + 1, 0)
                    load_shift(t, 2)
                    if more:
                        load_slice(t + 1, 1)
                if experts:
                    f = t - 1
                    sp.wait_ge(misc_done, job(t, "wt"))
                    apart(sp)
                    sp.dma_start(w_dram.rearrange("n c q -> c n q"), w_t[:, :]).then_inc(w_written, 16)
                    sp.wait_ge(w_written, f * 16 + 16)
                    for j in range(FJ):
                        src = bass.AP(w_dram.tensor, j * NJ * S, [[S, NJ], [0, PD], [1, S]])
                        sp.dma_start(w_rows[:, j, :], src).then_inc(w_loaded[j], 16)
                if attention:
                    load_shift(t, 3)
                    if more:
                        load_slice(t + 1, 2)
                        load_shift(t + 1, 0)
                if experts:
                    sp.wait_ge(dve_step, dve_at(t - 1, "cnorm"))
                    apart(sp)
                    sp.dma_start(out[t - 1].rearrange("(c p) e -> p c e", p=P), y_out[:]).then_inc(y_stored, 16)

            rounds(sp, round_)
            sp.wait_ge(y_stored, 16 * B + 1)

        @block.gpsimd
        def _(pool):
            def split_shift(t, g):
                n, m = t * G + g, neg_max[:, g % 2, :]
                pool.wait_ge(max_ready, n * (J * C) + J * C)
                if not (is0(t) and g == 0):
                    pool.wait_ge(misc_ready, shift_job(t, g - 1) if g else shift_job(t - 1, G - 1))
                    apart(pool)
                nc.gpsimd.tensor_copy(shift_parts[:, 0, :], m).then_inc(shift_chain, 1)
                pool.wait_ge(shift_chain, n * 3 + 1)
                nc.gpsimd.tensor_sub(shift_res[:], m, shift_parts[:, 0, :]).then_inc(shift_chain, 1)
                pool.wait_ge(shift_chain, n * 3 + 2)
                apart(pool)
                nc.gpsimd.tensor_copy(shift_parts[:, 1, :], shift_res[:]).then_inc(shift_chain, 1)
                pool.wait_ge(shift_chain, n * 3 + 3)
                nc.gpsimd.tensor_sub(shift_parts[:, 2, :], shift_res[:], shift_parts[:, 1, :]).then_inc(shift_split, 1)

            def fetch_values(t, g):
                if not is0(t):
                    pool.wait_ge(pv_done, (t - 1) * U + C * (g + 1))
                    apart(pool)
                nc.gpsimd.tensor_copy(v_cur[:, :, g * J:(g + 1) * J, 0:D],
                                      v_all[:, :, g * J:(g + 1) * J, t, :]).then_inc(v_ready, 1)

            def norm_scale(f, k, eps):
                pool.wait_ge(dve_step, dve_at(f, k + "mv"))
                apart(pool)
                nc.gpsimd.tensor_scalar(veps[:], mv[:, :, 1], eps, None, ALU.add).then_inc(pool_step, 1)
                pool.wait_ge(pool_step, pool_at(f, k + "eps"))
                nc.gpsimd.tensor_tensor(rstd[:], veps[:], minus_half[:], ALU.pow).then_inc(pool_step, 1)

            def weigh(f, t, j):
                pool.wait_ge(misc_done, job(t, f"down{j}"))
                pool.wait_ge(w_loaded[j], f * 16 + 16)
                nc.gpsimd.tensor_tensor(hid[:, j], hid[:, j], w_rows[:, j], ALU.mult).then_inc(pool_step, 1)

            nc.gpsimd.memset(ident[:], 0.0).then_inc(consts_made, 1)
            pool.wait_ge(consts_made, 1)
            nc.gpsimd.affine_select(out=ident[:], in_=ident[:], compare_op=ALU.not_equal, fill=1.0, base=0,
                                    pattern=[[-1, P]], channel_multiplier=1).then_inc(consts_made, 1)
            nc.gpsimd.memset(v_cur[:], 0.0).then_inc(consts_made, 1)
            nc.gpsimd.memset(minus_half[:], -0.5).then_inc(consts_made, 1)
            nc.gpsimd.memset(zeros[:], 0.0).then_inc(consts_made, 1)
            nc.gpsimd.memset(shift_parts[:], 0.0).then_inc(consts_made, 1)
            pool.wait_ge(consts_made, 6)
            nc.gpsimd.tensor_copy(ident_bf[:], ident[:]).then_inc(consts_made, 1)
            nc.gpsimd.memset(v_cur[:, :, :, D:D + 1], 1.0).then_inc(consts_made, 1)
            pool.wait_ge(consts_made, 8)
            pool.wait_ge(rows_loaded, 48)
            for b in range(B):
                pool.wait_ge(prep_mm, 4 * b + 1)
                nc.gpsimd.tensor_tensor(x_sb[:, b], x_sb[:, b], beta_sb[:].unsqueeze(1).to_broadcast([P, C, E]),
                                        ALU.add).then_inc(xb_ready, 1)
            for g in range(G):
                fetch_values(0, g)
            split_shift(0, 0)

            def round_(t, attention, experts, more):
                f = t - 1
                if attention and not is0(t):
                    fetch_values(t, G - 1)
                if experts:
                    pool.wait_ge(misc_done, job(t, "o3"))
                    nc.gpsimd.tensor_tensor(z[:].rearrange("p c (h d) -> p c h d", d=D),
                                            attn[:].rearrange("p c (h d) -> p c h d", d=D),
                                            bias_v[:, :, :, f, :], ALU.add).then_inc(pool_step, 1)
                if attention:
                    split_shift(t, 1)
                if experts:
                    norm_scale(f, "a", EPS_ATTENTION)
                    pool.wait_ge(dve_step, dve_at(f, "anorm"))
                    nc.gpsimd.tensor_tensor(z[:], z[:], gamma_sb[:].unsqueeze(1).to_broadcast([P, C, E]),
                                            ALU.mult).then_inc(pool_step, 1)
                    norm_scale(f, "b", EPS_LN)
                if attention:
                    if more:
                        fetch_values(t + 1, 0)
                    split_shift(t, 2)
                if experts:
                    pool.wait_ge(dve_step, dve_at(f, "top"))
                    nc.gpsimd.tensor_tensor(sdiff[:], sim[:], top[:, :, 0:1].to_broadcast([P, C, NE]),
                                            ALU.subtract).then_inc(pool_step, 1)
                if attention:
                    if more:
                        fetch_values(t + 1, 1)
                    split_shift(t, 3)
                if experts:
                    for j in range(FJ - 2):
                        weigh(f, t, j)
                if attention and more:
                    fetch_values(t + 1, 2)
                    split_shift(t + 1, 0)
                if experts:
                    for j in range(FJ - 2, FJ):
                        weigh(f, t, j)
                    norm_scale(f, "c", EPS_LN)

            rounds(pool, round_)

        @block.scalar
        def _(act):
            def copy(dst, src, scale=1.0):
                return nc.scalar.activation(dst, src, ACT.Copy, scale=scale)

            for dst, src in ((wq_sb, w_q), (wk_sb, w_k), (wv_sb, w_v)):
                act.dma_start(dst[:], src).then_inc(proj_loaded, 16)
            act.dma_start(gamma_sb[:], bass.AP(gamma.tensor, 0, [[0, P], [1, E]])).then_inc(rows_loaded, 16)
            act.dma_start(beta_sb[:], bass.AP(beta.tensor, 0, [[0, P], [1, E]])).then_inc(rows_loaded, 16)
            act.dma_start(scale_sb[:], bass.AP(ffn_scale.tensor, 0, [[0, P], [1, 1]])).then_inc(rows_loaded, 16)
            act.dma_start(hasher_sb[:], hasher_w).then_inc(keys_loaded, 16)
            act.dma_start(keys_sb[:], keys).then_inc(keys_loaded, 16)
            act.dma_start(down_sb[:], values_down.rearrange("n d p -> d n p")).then_inc(experts_loaded, 16)
            act.dma_start(up_sb[:], values_up.rearrange("(j n) p d -> (n p) j d", j=FJ)).then_inc(experts_loaded, 16)

            for b in range(B):
                act.wait_ge(prep_mm, 4 * b + 1)
                copy(x_t[:, b % 2, :], st_ps[:, b % 2, 0, :]).then_inc(prep_copied, 1)
                if b >= 2:
                    act.wait_ge(parts_written[b - 2], 2 * PARTS * 16)
                for a in range(2):
                    act.wait_ge(prep_mm, 4 * b + 2 + a)
                    copy(parts[:, b % 2, a, 0, :], (st_ps[:, b % 2, 1, :], sm_ps[:, b % 2, :])[a]).then_inc(prep_copied, 1)
                act.wait_ge(prep_mm, 4 * b + 4)
                copy(v_all[:, :, :, b, :].rearrange("p c h d -> p (c h) d"),
                     (ov_ps, mi_ps)[b % 2][:, :].rearrange("p (n d) -> p n d", d=D)).then_inc(prep_copied, 1)
            act.wait_ge(table_mm, 1)
            copy(rel_t[:], st_ps[:, 0, 0, :]).then_inc(table_copied, 1)
            act.wait_ge(table_mm, 2)
            copy(keys_t[:], ov_ps[0:PD, 0:NE]).then_inc(table_copied, 1)
            act.wait_ge(table_mm, 3)
            copy(sim_w[:], mi_ps[:, 0:NE]).then_inc(table_copied, 1)
            act.wait_ge(rows_loaded, 48)
            copy(half_scale[:], scale_sb[:], 0.5).then_inc(table_copied, 1)

            def bias_copy(g):
                act.wait_ge(bias_mm, g - CG + 2)
                if g >= CG + 2:
                    act.wait_ge(bias_turned, g - CG - 1)
                n = constant_from((g + 1) * J - 1) + 1
                turned = bias_t[:, g % 2, :].rearrange("p (a r) -> p r a", r=H)
                made = st_ps[:, 1, g % 2, 0:n * HPB].rearrange("p (r a) -> p r a", r=n)
                copy(turned[:, 0:n, :], made)
                copy(turned[:, n:, :], made[:, n - 1:n, :].to_broadcast([P, H - n, HPB])).then_inc(bias_copied, 1)

            def bias_keep(g):
                act.wait_ge(bias_turned, g - CG + 1)
                copy(bias_v[:, :, g * J:(g + 1) * J].rearrange("p c j b d -> p c (j b d)"),
                     st_ps[:, 0, g % 2, :].rearrange("p (c n) -> p c n", c=C)).then_inc(bias_kept, 1)

            def bias_spread():
                act.wait_ge(bias_mm, 1)
                n = CG * J * B * D
                copy(bias_v[:, :, 0:CG * J].rearrange("p c h b d -> p c (h b d)"),
                     mi_ps[:, 0:n].unsqueeze(1).to_broadcast([P, C, n])).then_inc(bias_kept, 1)

            def shift_copy(t, g):
                act.wait_ge(misc_ready, shift_job(t, g))
                if not (is0(t) and g == 0):
                    act.wait_ge(shift_loaded[(g - 1) % G], 16 * (t if g == 0 else t + 1))
                copy(shift_rows[:, :], mi_bf[0:PARTS * J * C, 0:P]).then_inc(misc_done, 1)

            mi_bf = mi_ps[:, :].bitcast(BF16)
            bias_spread()
            for g in range(CG, G):
                bias_copy(g)
                if g > CG:
                    bias_keep(g - 1)
            bias_keep(G - 1)
            shift_copy(0, 0)

            def exps(t, u):
                n = t * U + u
                for half in range(2):
                    act.wait_ge(scores_ready, 2 * n + half + 1)
                    if half == 0 and not (is0(t) and u < 2):
                        act.wait_ge(pv_done, n - 1)
                    nc.scalar.activation(probs[:, u % 2, 2 * half:2 * half + 2, :], st_ps[:, half], ACT.Exp,
                                         scale=SCORE_SCALE).then_inc(probs_ready, 1)

            def o_copy(t, g):
                act.wait_ge(pv_done, t * U + C * (g + 1))
                if not (is0(t) and g == 0):
                    act.wait_ge(misc_ready, job(t, f"o{g - 1}") if g else job(t, f"o{G - 1}"))
                copy(o_sb[:], ov_ps[:]).then_inc(o_copied, 1)

            def expert_copy(t, name):
                f = t - 1
                act.wait_ge(misc_ready, job(t, name))
                if name == "x1t":
                    copy(x1_t[:], mi_ps[:]).then_inc(misc_done, 1)
                elif name == "sim":
                    copy(sim[:].rearrange("p c n -> p (c n)"), mi_ps[:, 0:C * NE]).then_inc(misc_done, 1)
                elif name == "wt":
                    copy(w_t[:], mi_ps[:, 0:P]).then_inc(misc_done, 1)
                elif name.startswith("down"):
                    j = int(name[4:])
                    nc.scalar.activation(tanh_sb[:, j % 2, :], mi_ps[:], ACT.Tanh, scale=0.5).then_inc(act_step, 1)

            def round_(t, attention, experts, more):
                for u in range(U):
                    if attention:
                        exps(t, u)
                    if u == 0 and experts:
                        o_copy(t - 1, G - 1)
                    if u and u % C == 0 and attention:
                        o_copy(t, u // C - 1)
                    if u == 6 and experts:
                        act.wait_ge(pool_step, pool_at(t - 1, "sdiff"))
                        nc.scalar.activation(sexp[:], sdiff[:], ACT.Exp).then_inc(act_step, 1)
                    for half in JOBS.get(u, ([], [])):
                        for name in half:
                            if name.startswith("shift") and attention and (more or name != "shift0"):
                                shift_copy(*((t, int(name[5:])) if name != "shift0" else (t + 1, 0)))
                            elif name not in OWN and name not in ("o3", "up") and experts:
                                expert_copy(t, name)

            rounds(act, round_)

        @block.vector
        def _(dve):
            two_ones = 1.0019378662109375
            nc.vector.memset(k_stack[64:P].bitcast(F32), two_ones).then_inc(stack_set, 1)
            nc.vector.memset(q_stack[64:P].bitcast(F32), 0.0).then_inc(stack_set, 1)

            for b in range(B):
                for a in range(2):
                    n = 3 * (2 * b + a)
                    hi, mid, lo = (parts[:, b % 2, a, i, :] for i in range(PARTS))
                    dve.wait_ge(prep_copied, 4 * b + 2 + a)
                    nc.vector.tensor_sub(resid[:, a], (st_ps[:, b % 2, 1, :], sm_ps[:, b % 2, :])[a], hi) \
                      .then_inc(prep_split, 1)
                    dve.wait_ge(prep_split, n + 1)
                    nc.vector.tensor_copy(mid, resid[:, a]).then_inc(prep_split, 1)
                    dve.wait_ge(prep_split, n + 2)
                    nc.vector.tensor_sub(lo, resid[:, a], mid).then_inc(prep_split, 1)

            def maximum(t, pos, c):
                n, g = t * U + pos, (pos // J) % G
                dve.wait_ge(sm_ready, C * n + c + 1)
                if pos % J == 0 and c == 0 and not (is0(t) and pos // J < 2):
                    dve.wait_ge(shift_split, t * G + pos // J - 1)
                col = (pos % J) * C + c
                nc.vector.tensor_reduce(neg_max[:, g % 2, col:col + 1], sm_ps[:, c % 2, :], AX.X, ALU.max,
                                        negate=True).then_inc(max_ready, 1)

            for pos in range(LEAD):
                for c in range(C):
                    maximum(0, pos, c)

            def attend(t, name, g):
                dve.wait_ge(misc_ready, name)
                o = mi_ps[:].rearrange("p (c j w) -> p c j w", c=C, j=J)
                n = t * G + g
                nc.vector.reciprocal(rsum[:], o[:, :, :, D]).then_inc(rsum_ready, 1)
                dve.wait_ge(rsum_ready, n + 1)
                nc.vector.tensor_tensor(attn[:, :, g * J * D:(g + 1) * J * D].rearrange("p c (j d) -> p c j d", d=D),
                                        o[:, :, :, 0:D], rsum[:].unsqueeze(3).to_broadcast([P, C, J, D]),
                                        ALU.mult).then_inc(misc_done, 1)

            def stats_of(f, k, src):
                for c in range(C):
                    i = nc.vector.bn_stats(stats[:, c, :], src[:, c, :])
                i.then_inc(dve_step, 1)

            def mv_of(f, k):
                dve.wait_ge(dve_step, dve_at(f, k + "stats"))
                apart(dve)
                for c in range(C):
                    i = nc.vector.bn_aggr(mv[:, c, :], stats[:, c, :])
                i.then_inc(dve_step, 1)

            def norm_of(f, k, dst, src):
                dve.wait_ge(pool_step, pool_at(f, k + "pow"))
                for c in range(C):
                    i = nc.vector.tensor_scalar(dst[:, c, :], src[:, c, :], mv[:, c, 0:1], rstd[:, c:c + 1],
                                                ALU.subtract, ALU.mult)
                i.then_inc(dve_step, 1)

            def after(f, name):
                dve.wait_ge(dve_step, dve_at(f, name))

            def step(i):
                i.then_inc(dve_step, 1)

            def flat(a):
                return a[:].rearrange("p c n -> p (c n)")

            def hidden(t, j):
                dve.wait_ge(act_step, act_at(t - 1, f"tanh{j}"))
                nc.vector.scalar_tensor_tensor(out=hid[:, j], in0=tanh_sb[:, j % 2, :], scalar=1.0, in1=mi_ps[:],
                                               op0=ALU.add, op1=ALU.mult).then_inc(misc_done, 1)

            def expert_steps(t, u, s):
                f = t - 1
                at = (u, s)
                if at == (1, 1):
                    attend(f, job(t, "o3"), G - 1)
                elif at == (2, 0):
                    dve.wait_ge(pool_step, pool_at(f, "bias"))
                    stats_of(f, "a", z)
                elif at == (2, 2):
                    mv_of(f, "a")
                elif at == (3, 0):
                    norm_of(f, "a", z, z)
                elif at == (3, 3):
                    dve.wait_ge(pool_step, pool_at(f, "gamma"))
                    step(nc.vector.tensor_tensor(z[:], z[:], x_sb[:, f], ALU.add))
                elif at == (4, 0):
                    after(f, "resid")
                    stats_of(f, "b", z)
                elif at == (4, 1):
                    mv_of(f, "b")
                elif at == (4, 3):
                    norm_of(f, "b", x1, z)
                elif at == (6, 1):
                    dve.wait_ge(misc_done, job(t, "sim"))
                    apart(dve)
                    for c in range(C):
                        i = nc.vector.max(top[:, c, :], sim[:, c, :])
                    step(i)
                elif at == (6, 2):
                    after(f, "top")
                    fourth = top[:, :, TOPK - 1:TOPK].to_broadcast([P, C, NE])
                    step(nc.vector.tensor_tensor(above[:], sim[:], fourth, ALU.is_gt))
                    step(nc.vector.tensor_tensor(ties[:], sim[:], fourth, ALU.is_equal))
                elif at == (6, 3):
                    after(f, "above")
                    step(nc.vector.tensor_reduce(n_above[:], above[:], AX.X, ALU.add))
                elif at == (7, 0):
                    hidden(t, 0)
                elif at == (7, 1):
                    after(f, "n_above")
                    for c in range(C):
                        i = nc.vector.tensor_tensor_scan(rank[:, c, :], ties[:, c, :], zeros[:], n_above[:, c:c + 1],
                                                         ALU.add, ALU.add)
                    step(i)
                elif at == (7, 2):
                    after(f, "rank")
                    step(nc.vector.scalar_tensor_tensor(out=flat(keep), in0=flat(rank), scalar=float(TOPK),
                                                        in1=flat(ties), op0=ALU.is_le, op1=ALU.mult))
                elif at == (7, 3):
                    after(f, "keep")
                    step(nc.vector.tensor_tensor(mask[:], keep[:], above[:], ALU.add))
                elif at == (8, 0):
                    hidden(t, 1)
                elif at == (8, 1):
                    after(f, "mask")
                    dve.wait_ge(act_step, act_at(f, "sexp"))
                    step(nc.vector.tensor_tensor(wexp[:], sexp[:], mask[:], ALU.mult))
                elif at == (8, 2):
                    after(f, "wexp")
                    step(nc.vector.tensor_reduce(wsum[:], wexp[:], AX.X, ALU.add))
                elif at == (8, 3):
                    after(f, "wsum")
                    step(nc.vector.reciprocal(winv[:], wsum[:]))
                    after(f, "winv")
                    step(nc.vector.tensor_scalar(wscale[:], winv[:], half_scale[:, 0:1], None, ALU.mult))
                elif at == (9, 0):
                    after(f, "wscale")
                    step(nc.vector.tensor_tensor(w_tok[:], wexp[:], wscale[:].unsqueeze(2).to_broadcast([P, C, NE]),
                                                 ALU.mult))
                    hidden(t, 2)
                elif s == 0 and 10 <= u <= 14:
                    hidden(t, u - 7)
                elif at == (15, 0):
                    dve.wait_ge(misc_ready, job(t, "up"))
                    nc.vector.scalar_tensor_tensor(out=flat(y), in0=flat(x1), scalar=2.0, in1=mi_ps[:],
                                                   op0=ALU.mult, op1=ALU.add).then_inc(misc_done, 1)
                elif at == (15, 1):
                    dve.wait_ge(misc_done, job(t, "up"))
                    stats_of(f, "c", y)
                elif at == (15, 2):
                    mv_of(f, "c")
                elif at == (15, 3):
                    dve.wait_ge(y_stored, f * 16 + 1)
                    norm_of(f, "c", y_out, y)

            def round_(t, attention, experts, more):
                for u in range(U):
                    for s in range(C):
                        if attention and (more or u + LEAD < U):
                            maximum(t, u + LEAD, s)
                        if attention and s == 1 and u in (5, 9, 13):
                            attend(t, job(t, f"o{u // C - 1}"), u // C - 1)
                        if experts:
                            expert_steps(t, u, s)

            rounds(dve, round_)

        @block.tensor
        def _(pe):
            mi_bf = mi_ps[:, :].bitcast(BF16)
            pitch = rel_t[:, :].ap[0][0]

            def prep(b):
                if b == 0:
                    pe.wait_ge(consts_made, 2)
                pe.wait_ge(x_loaded[b], 16)
                if b >= 2:
                    pe.wait_ge(prep_copied, 4 * (b - 2) + 4)
                    pe.wait_ge(prep_split, 3 * (2 * (b - 2) + 1) + 1)
                for c in range(C):
                    i = nc.tensor.transpose(st_ps[:, b % 2, 0, c * P:(c + 1) * P], x_sb[:, b, c, :], ident[:])
                i.then_inc(prep_mm, 1)
                if b == 0:
                    pe.wait_ge(proj_loaded, 48)
                pe.wait_ge(prep_copied, 4 * b + 1)
                xt = x_t[:, b % 2, :]
                nc.tensor.matmul(st_ps[:, b % 2, 1, :], wq_sb[:], xt, start=True, stop=True).then_inc(prep_mm, 1)
                nc.tensor.matmul(sm_ps[:, b % 2, :], wk_sb[:], xt, start=True, stop=True).then_inc(prep_mm, 1)
                for c in range(C):
                    i = nc.tensor.matmul((ov_ps, mi_ps)[b % 2][:, c * P:(c + 1) * P], xt[:, c * P:(c + 1) * P],
                                         wv_sb[:], start=True, stop=True)
                i.then_inc(prep_mm, 1)

            def maximum_scores(t, pos, c):
                n, h = t * U + pos, pos % U
                k = C * n + c
                if pos % J == 0 and c == 0:
                    pe.wait_ge(stack_loaded[pos // J % G], 32 * (t + pos // U) + 32)
                if not (is0(t) and pos == 0 and c < 2):
                    pe.wait_ge(max_ready, k - 1)
                nc.tensor.matmul(sm_ps[:, c % 2, :], q_stack[0:SHIFT_ROW, h, c * P:(c + 1) * P],
                                 k_stack[0:SHIFT_ROW, h, :], start=True, stop=True).then_inc(sm_ready, 1)

            def scores(t, u, half):
                n, g, kc = t * U + u, u // C, u % C
                if half == 0 and kc == 0:
                    pe.wait_ge(shift_loaded[g], 16 * t + 16)
                if not (is0(t) and u == 0):
                    pe.wait_ge(probs_ready, 2 * n + half - 1)
                for jj in range(2):
                    h = g * J + 2 * half + jj
                    i = nc.tensor.matmul(st_ps[:, half, jj, :], k_stack[:, h, kc * P:(kc + 1) * P], q_stack[:, h, :],
                                         start=True, stop=True)
                i.then_inc(scores_ready, 1)

            def values(t, u):
                n, g, kc = t * U + u, u // C, u % C
                if kc == 0:
                    pe.wait_ge(v_ready, t * G + g + 1)
                    if not (is0(t) and g == 0):
                        pe.wait_ge(o_copied, t * G + g)
                pe.wait_ge(probs_ready, 2 * n + 2)
                for j in range(J):
                    i = nc.tensor.matmul(ov_ps[j * TILE:(j + 1) * TILE, :], v_cur[:, kc, g * J + j, :],
                                         probs[:, u % 2, j, :], start=(kc == 0), stop=(kc == C - 1))
                i.then_inc(pv_done, 1)

            def turn(dst, src, idn):
                return nc.tensor.transpose(dst, src, idn)

            def misc(t, name):
                f = t - 1
                pe.wait_ge(misc_done, job(t, name) - 1)
                if name.startswith("o"):
                    g = int(name[1:])
                    pe.wait_ge(o_copied, (f if g == G - 1 else t) * G + g + 1)
                    for c in range(C):
                        i = turn(mi_ps[:, c * P:(c + 1) * P], o_sb[:, c * P:(c + 1) * P], ident[:])
                elif name.startswith("shift"):
                    g = int(name[5:])
                    pe.wait_ge(shift_split, (t + 1 if g == 0 else t) * G + g + 1)
                    i = turn(mi_bf[:, 0:P], shift_parts[:].rearrange("p i n -> p (i n)"), ident_bf[:])
                elif name == "x1t":
                    pe.wait_ge(dve_step, dve_at(f, "bnorm"))
                    for c in range(C):
                        i = turn(mi_ps[:, c * P:(c + 1) * P], x1[:, c, :], ident[:])
                elif name == "sim":
                    for c in range(C):
                        i = nc.tensor.matmul(mi_ps[:, c * NE:(c + 1) * NE], x1_t[:, c * P:(c + 1) * P], sim_w[:],
                                             start=True, stop=True)
                elif name == "wt":
                    pe.wait_ge(dve_step, dve_at(f, "w"))
                    i = turn(mi_ps[:, 0:P], w_tok[:].rearrange("p c n -> p (c n)"), ident[:])
                elif name == "up":
                    for j in range(FJ):
                        pe.wait_ge(pool_step, pool_at(f, f"weigh{j}"))
                        for c in range(C):
                            i = nc.tensor.matmul(mi_ps[:, c * P:(c + 1) * P], hid[:, j, c * P:(c + 1) * P], up_sb[:, j, :],
                                                 start=(j == 0 and c == 0), stop=(j == FJ - 1), skip_group_check=True)
                else:
                    j = int(name[4:])
                    i = nc.tensor.matmul(mi_ps[:], down_sb[:, j * NJ:(j + 1) * NJ, :], x1_t[:], start=True, stop=True)
                i.then_inc(misc_ready, 1)

            for b in range(B):
                prep(b)
            pe.wait_ge(rel_loaded, 16)
            pe.wait_ge(prep_copied, 4 * (B - 1) + 4)
            pe.wait_ge(prep_split, 3 * (2 * B - 1) + 1)
            for n in range(NWIN // P):
                i = turn(st_ps[:, 0, 0, n * P:(n + 1) * P], rel_win[:, n, :], ident[:])
            i.then_inc(table_mm, 1)
            pe.wait_ge(keys_loaded, 32)
            turn(ov_ps[0:PD, 0:NE], keys_sb[:], ident[0:NE, 0:NE]).then_inc(table_mm, 1)
            pe.wait_ge(table_copied, 2)
            nc.tensor.matmul(mi_ps[:, 0:NE], hasher_sb[:], keys_t[:], start=True, stop=True).then_inc(table_mm, 1)

            early = [(pos, c) for pos in range(LEAD) for c in range(C)]

            def early_maxima(n):
                for _ in range(n):
                    if early:
                        maximum_scores(0, *early.pop(0))

            pe.wait_ge(table_copied, 3)
            for kc in range(C):
                i = nc.tensor.matmul(mi_ps[:, 0:CG * J * B * D], rel_t[:, LAST:LAST + P],
                                     v_all[:, kc, 0:CG * J].rearrange("p h b d -> p (h b d)"),
                                     start=(kc == 0), stop=(kc == C - 1))
                early_maxima(1)
            i.then_inc(bias_mm, 1)

            def bias_turn(g):
                pe.wait_ge(bias_copied, g - CG + 1)
                if g >= CG + 2:
                    pe.wait_ge(bias_kept, g - CG)
                for c in range(C):
                    i = turn(st_ps[:, 0, g % 2, c * P:(c + 1) * P], bias_t[:, g % 2, c * P:(c + 1) * P], ident[:])
                i.then_inc(bias_turned, 1)

            for g in range(CG, G):
                if g >= CG + 2:
                    pe.wait_ge(bias_copied, g - CG - 1)
                n = constant_from((g + 1) * J - 1) + 1
                for kc in range(C):
                    for j in range(J):
                        h = g * J + j
                        window = bass.AP(rel_t, S - 1 - HPB * h + (P // H) * kc, [[pitch, P], [HPB, n], [-1, HPB]])
                        i = nc.tensor.matmul(st_ps[j * TILE:(j + 1) * TILE, 1, g % 2, 0:n * HPB], v_all[:, kc, h].rearrange("p b d -> p (b d)"),
                                             window, start=(kc == 0), stop=(kc == C - 1))
                    if kc == C - 1:
                        i.then_inc(bias_mm, 1)
                    early_maxima(1)
                if g > CG:
                    bias_turn(g - 1)
            bias_turn(G - 1)
            early_maxima(J * C + 2 - (LEAD * C - len(early)))
            pe.wait_ge(bias_kept, 1)
            pe.wait_ge(consts_made, 8)
            pe.wait_ge(shift_split, 1)
            turn(mi_bf[:, 0:P], shift_parts[:].rearrange("p i n -> p (i n)"), ident_bf[:]) \
                .then_inc(misc_ready, 1)
            early_maxima(len(early))
            pe.wait_ge(bias_kept, G - CG + 1)
            pe.wait_ge(experts_loaded, 32)

            def round_(t, attention, experts, more):
                for u in range(U):
                    before, behind = JOBS.get(u, ([], []))

                    def here(n):
                        return (attention if n in OWN else experts) and (more or n != "shift0")
                    maxima = attention and (more or u + LEAD < U)
                    if maxima:
                        maximum_scores(t, u + LEAD, 0)
                    if attention:
                        scores(t, u, 0)
                    if maxima:
                        maximum_scores(t, u + LEAD, 1)
                    if attention:
                        scores(t, u, 1)
                    for name in before:
                        if here(name):
                            misc(t, name)
                    if u and attention:
                        values(t, u - 1)
                    elif u == 0 and experts:
                        values(t - 1, U - 1)
                    if maxima:
                        maximum_scores(t, u + LEAD, 2)
                    for name in behind:
                        if here(name):
                            misc(t, name)
                    if maxima:
                        maximum_scores(t, u + LEAD, 3)

            rounds(pe, round_)


_INS = ["L0_attn_x", "L0_attn_Wq", "L0_attn_Wk", "L0_attn_Wv", "L0_attn_rel_table", "L0_attn_gamma", "L0_attn_beta",
        "L0_ffn_hasher_w", "L0_ffn_keys", "L0_ffn_values_down", "L0_ffn_values_up", "L0_ffn_scale"]


def kernel(**inputs):
    import numpy as np
    import concourse.bacc as bacc
    from concourse import mybir as _mybir
    from concourse.bass_utils import run_bass_kernel_spmd

    nc = bacc.Bacc("TRN2", target_bir_lowering=False, num_devices=1)
    arrays, args = {}, []
    for name in _INS:
        a = np.ascontiguousarray(inputs[name])
        arrays[name] = a
        args.append(nc.dram_tensor(name, a.shape, _mybir.dt.from_np(a.dtype), kind="ExternalInput").ap())
    shape = arrays["L0_attn_x"].shape
    args.append(nc.dram_tensor("out", shape, _mybir.dt.float32, kind="ExternalOutput").ap())
    bass_postln_attention_product_key_ffn(nc, *args)
    return run_bass_kernel_spmd(nc, [arrays], core_ids=[0]).results[0]["out"]
```

```python
import concourse.bass as bass
from concourse import mybir
from contextlib import ExitStack


def bass_postln_attention_product_key_ffn(nc, x, w_q, w_k, w_v, rel_table, gamma, beta,
                                          hasher_w, keys, values_down, values_up, ffn_scale, out):
    F32, BF16 = mybir.dt.float32, mybir.dt.bfloat16
    ALU, ACT, AX = mybir.AluOpType, mybir.ActivationFunctionType, mybir.AxisListType

    B, S, E = x.shape
    H = rel_table.shape[1]
    D = E // H
    P = 128
    C = S // P
    J = 4
    G = H // J
    U = G * C
    NE, PD = keys.shape
    NJ = P // PD
    FJ = NE // NJ
    TOPK = 4
    PARTS = 3
    TERMS = PARTS * PARTS * D
    SHIFT_ROW = 96
    SCORE_SCALE = float(E) ** -0.5
    LEAD = 7
    HPB = S // H
    LAST = rel_table.shape[0] - 1
    NWIN = S
    TILE = 32
    EPS_ATTENTION, EPS_LN = 1e-3, 1e-5

    def constant_from(h):
        return min(max(-(-(LAST - S + HPB + HPB * h) // HPB), 0), H)

    CG = sum(constant_from((g + 1) * J - 1) == 0 for g in range(G))
    assert B % 2 == 0 and CG == G - 2
    assert all(S - 1 - HPB * g * J + (C - 1) * P // H + HPB * constant_from((g + 1) * J - 1) < NWIN
               for g in range(CG, G)) and NWIN - P >= LAST and constant_from(H - 1) < H

    ctx = ExitStack()
    with ctx:
        def sb(name, shape, dt=F32):
            return ctx.enter_context(nc.sbuf_tensor(name, shape, dt))

        def pb(name, shape, dt=F32):
            return ctx.enter_context(nc.psum_tensor(name, shape, dt))

        def sem(name):
            return ctx.enter_context(nc.semaphore(name))

        ident, ident_bf = sb("ident", [P, P]), sb("ident_bf", [P, P], BF16)
        minus_half, zeros = sb("minus_half", [P, C]), sb("zeros", [P, NE])
        wq_sb, wk_sb, wv_sb = sb("wq_sb", [P, E]), sb("wk_sb", [P, E]), sb("wv_sb", [P, E])
        gamma_sb, beta_sb = sb("gamma_sb", [P, E]), sb("beta_sb", [P, E])
        hasher_sb, keys_sb, keys_t = sb("hasher_sb", [PD, E]), sb("keys_sb", [NE, PD]), sb("keys_t", [PD, NE])
        sim_w = sb("sim_w", [P, NE])
        down_sb = sb("down_sb", [P, NE, PD])
        up_sb = sb("up_sb", [P, FJ, E])
        scale_sb, half_scale = sb("scale_sb", [P, 1]), sb("half_scale", [P, 1])
        rel_win = sb("rel_win", [P, NWIN // P, P])
        rel_t = sb("rel_t", [P, NWIN])
        x_sb = sb("x_sb", [P, B, C, E])
        x_t = sb("x_t", [P, 2, S])
        parts = sb("parts", [P, B, 2, PARTS, S], BF16)
        resid = sb("resid", [P, 2, S])
        v_all = sb("v_all", [P, C, H, B, D])
        v_cur = sb("v_cur", [P, C, H, TILE])
        q_stack, k_stack = sb("q_stack", [P, H, S], BF16), sb("k_stack", [P, H, S], BF16)
        neg_max = sb("neg_max", [P, 2, J * C])
        shift_parts = sb("shift_parts", [P, P // (J * C), J * C], BF16)
        shift_res = sb("shift_res", [P, J * C])
        shift_rows = sb("shift_rows", [PARTS * J * C, P], BF16)
        probs = sb("probs", [P, 2, J, S])
        o_sb = sb("o_sb", [P, S])
        rsum = sb("rsum", [P, C, J])
        attn = sb("attn", [P, C, E])
        bias_t = sb("bias_t", [P, 2, S])
        bias_v = sb("bias_v", [P, C, H, B, D])
        z = sb("z", [P, C, E])
        stats, mv = sb("stats", [P, C, 6]), sb("mv", [P, C, 2])
        veps, rstd = sb("veps", [P, C]), sb("rstd", [P, C])
        x1, x1_t = sb("x1", [P, C, E]), sb("x1_t", [P, S])
        sim, top = sb("sim", [P, C, NE]), sb("top", [P, C, 8])
        sdiff, sexp = sb("sdiff", [P, C, NE]), sb("sexp", [P, C, NE])
        above, ties, rank = sb("above", [P, C, NE]), sb("ties", [P, C, NE]), sb("rank", [P, C, NE])
        keep, mask, wexp = sb("keep", [P, C, NE]), sb("mask", [P, C, NE]), sb("wexp", [P, C, NE])
        n_above, wsum, winv, wscale = sb("n_above", [P, C]), sb("wsum", [P, C]), sb("winv", [P, C]), sb("wscale", [P, C])
        w_tok, w_t = sb("w_tok", [P, C, NE]), sb("w_t", [P, P])
        w_rows = sb("w_rows", [P, FJ, S])
        tanh_sb = sb("tanh_sb", [P, 3, S])
        hid = sb("hid", [P, FJ, S])
        y, y_out = sb("y", [P, C, E]), sb("y_out", [P, C, E])

        st_ps = pb("st_ps", [P, 3, S])
        sm_ps = pb("sm_ps", [P, 2, S])
        ov_ps = pb("ov_ps", [P, S])
        mi_ps = pb("mi_ps", [P, S])
        si_ps = pb("si_ps", [P, S])

        stack_dram = nc.dram_tensor("stack_dram", [B, 2, H, D * PARTS * PARTS, S], BF16, kind="Internal").ap()
        rel_dram = nc.dram_tensor("rel_dram", [NWIN + P // H, H], F32, kind="Internal").ap()
        w_dram = nc.dram_tensor("w_dram", [NE, C, P], F32, kind="Internal").ap()

        waits_met = sem("waits_met")
        consts_made, stack_set = sem("consts_made"), sem("stack_set")
        x_loaded = [sem(f"x_loaded{b}") for b in range(B)]
        proj_loaded, rows_loaded, beta_loaded = sem("proj_loaded"), sem("rows_loaded"), sem("beta_loaded")
        rel_written, rel_loaded = sem("rel_written"), sem("rel_loaded")
        keys_loaded, experts_loaded = sem("keys_loaded"), sem("experts_loaded")
        prep_mm, prep_copied, prep_split = sem("prep_mm"), sem("prep_copied"), sem("prep_split")
        first_written = sem("first_written")
        parts_written = [sem(f"parts_written{b}") for b in range(B)]
        stack_loaded = [sem(f"stack_loaded{g}") for g in range(G)]
        shift_loaded = [sem(f"shift_loaded{g}") for g in range(G)]
        table_mm, table_copied = sem("table_mm"), sem("table_copied")
        bias_mm, bias_copied, bias_turned, bias_kept = (
            sem("bias_mm"), sem("bias_copied"), sem("bias_turned"), sem("bias_kept"))
        scores_ready, probs_ready, pv_done = sem("scores_ready"), sem("probs_ready"), sem("pv_done")
        sm_ready, max_ready = sem("sm_ready"), sem("max_ready")
        shift_chain, shift_split = sem("shift_chain"), sem("shift_split")
        v_ready, o_copied, rsum_ready = sem("v_ready"), sem("o_copied"), sem("rsum_ready")
        xb_ready = sem("xb_ready")
        misc_ready, misc_done, hidden_made = sem("misc_ready"), sem("misc_done"), sem("hidden_made")
        side_ready, side_done = sem("side_ready"), sem("side_done")
        dve_step, pool_step, act_step = sem("dve_step"), sem("pool_step"), sem("act_step")
        w_loaded = [sem(f"w_loaded{j}") for j in range(FJ)]
        weighed, tail_weighed = sem("weighed"), sem("tail_weighed")
        w_written, y_made, y_stored = sem("w_written"), sem("y_made"), sem("y_stored")

        JOBS = {0: ([], ["o3"]), 2: (["shift1"], []), 4: ([], ["o0"]), 5: ([], ["x1t"]),
                6: (["sim", "shift2"], ["down0"]), 7: ([], ["down1"]), 8: ([], ["o1", "down2"]),
                9: (["shift3"], ["wt", "down3"]), 10: ([], ["down4"]), 11: (["up0"], ["down5"]),
                12: (["up1", "up2"], ["down6"]), 13: (["up3", "up4"], ["down7"]),
                14: (["shift0", "up5"], ["o2", "up6", "up7"])}
        OWN = ("shift0", "shift1", "shift2", "shift3", "o0", "o1", "o2")
        SIDE = ("o3", "o0", "x1t", "sim", "o1", f"up{FJ - 1}")

        def is_misc(n):
            return n[:2] != "up" and n not in SIDE

        def is_kept(n):
            return is_misc(n) and n[:4] != "down"

        def is_side(n):
            return n in SIDE

        def here(n, attention, experts, more):
            return (attention if n in OWN else experts) and (more or n != "shift0")

        def job(t, name, counted):
            first, every, last, tail = (
                [n for u in sorted(JOBS) for half in JOBS[u] for n in half if here(n, *kind) and (counted(n) or n == name)]
                for kind in ((True, False, True), (True, True, True), (True, True, False), (False, True, False)))
            own = 1 if counted(name) else 0
            many = [len([n for n in names if counted(n)]) for names in (first, every, last)]
            prologue = 0 if counted is is_side else 1
            if isinstance(t, int) and t == 0:
                return prologue + first.index(name) + own
            if isinstance(t, int) and t == B:
                return prologue + many[0] + (B - 2) * many[1] + many[2] + tail.index(name) + own
            names = last if isinstance(t, int) and t == B - 1 else every
            return (t - 1) * many[1] + (prologue + many[0] + names.index(name) + own)

        def shift_job(t, g, counted):
            if g:
                return job(t, f"shift{g}", counted)
            return 1 if isinstance(t, int) and t == 0 else job(t - 1, "shift0", counted)

        TAIL_VECTOR = [j for j in range(FJ) if j % 3 != 2]
        TAIL_POOL = [j for j in range(FJ) if j % 3 == 2]

        def hidden_count(f, j):
            return f * FJ + (j + 1)

        def down_bank(t, j):
            return st_ps[:, j % 3, :] if isinstance(t, int) and t == B else mi_ps[:, :]

        def score_bank(k):
            return 1 if k == U * J - 1 else k % 3

        def scores_since(k):
            return next(n for n in range(1, 5) if score_bank((k - n) % (U * J)) == score_bank(k))

        DVE_STEPS = ["astats", "amv", "bstats", "bmv", "top", "above", "ties", "n_above", "rank", "keep", "mask",
                     "wexp", "wsum", "winv", "wscale", "w", "cstats", "cmv"]
        POOL_STEPS = ["bias", "aeps", "acentre", "apow", "ascale", "gamma", "resid", "beps", "bcentre", "bpow",
                      "bscale", "sdiff", "ceps", "ccentre", "cpow"]
        ACT_STEPS = ["tanh0", "sexp"] + [f"tanh{j}" for j in range(1, FJ)]

        def dve_at(f, name):
            return f * len(DVE_STEPS) + (DVE_STEPS.index(name) + 1)

        def pool_at(f, name):
            return f * len(POOL_STEPS) + (POOL_STEPS.index(name) + 1)

        def act_at(f, name):
            return f * len(ACT_STEPS) + (ACT_STEPS.index(name) + 1)

        def prep_banks(b):
            return [(st_ps[:, 0, :], st_ps[:, 1, :], st_ps[:, 2, :]), (ov_ps[:, :], mi_ps[:, :], si_ps[:, :])][b % 2]

        def bias_banks(g):
            return [(st_ps[:, 0, :], st_ps[:, 2, :]), (st_ps[:, 1, :], st_ps[:, 0, :])][(g - CG) % 2]

        def is0(t):
            return isinstance(t, int) and t == 0

        def apart(engine):
            engine.sem_inc(waits_met, 1)

        def rounds(engine, round_):
            round_(0, True, False, True)
            with engine.Fori(1, B - 1) as t:
                round_(t, True, True, True)
            round_(B - 1, True, True, False)
            round_(B, False, True, False)

        block = ctx.enter_context(nc.Block())

        @block.sync
        def _(sp):
            def load_slice(t, g):
                if not is0(t):
                    sp.wait_ge(scores_ready, (t - 1) * (J * U) + J * C * (g + 1))
                    apart(sp)
                for a, stack in enumerate((q_stack, k_stack)):
                    src = stack_dram[t, a, g * J:(g + 1) * J]
                    sp.dma_start(stack[0:TERMS, g * J:(g + 1) * J, :], src.rearrange("h r s -> r h s")) \
                      .then_inc(stack_loaded[g], 16)

            def load_shift(t, g):
                sp.wait_ge(misc_done, shift_job(t, g, is_kept))
                sp.dma_start(q_stack[SHIFT_ROW:SHIFT_ROW + PARTS, g * J:(g + 1) * J, :]
                             .rearrange("i h (c q) -> i (h c) q", c=C), shift_rows[:, :]).then_inc(shift_loaded[g], 16)

            sp.sem_inc(y_stored, 1)
            for b in range(B):
                sp.dma_start(x_sb[:, b], x[b].rearrange("(c p) e -> p c e", p=P)).then_inc(x_loaded[b], 16)
                if b == 0:
                    for dst, src in ((wq_sb, w_q), (wk_sb, w_k), (wv_sb, w_v)):
                        sp.dma_start(dst[:], src).then_inc(proj_loaded, 16)
            sp.dma_start(beta_sb[:], bass.AP(beta.tensor, 0, [[0, P], [1, E]])).then_inc(beta_loaded, 16)
            sp.dma_start(rel_dram[0:LAST + 1, :], rel_table).then_inc(rel_written, 16)
            sp.dma_start(rel_dram[LAST + 1:, :],
                         bass.AP(rel_table.tensor, LAST * H, [[0, NWIN + P // H - LAST - 1], [1, H]])).then_inc(rel_written, 16)
            sp.wait_ge(rel_written, 32)
            sp.dma_start(rel_win[:], bass.AP(rel_dram.tensor, 0, [[H, P], [H * P, NWIN // P], [1, P]])) \
              .then_inc(rel_loaded, 16)
            sp.dma_start(hasher_sb[:], hasher_w).then_inc(keys_loaded, 16)
            sp.dma_start(keys_sb[:], keys).then_inc(keys_loaded, 16)
            R = J * D
            for a in range(2):
                sp.wait_ge(prep_split, 3 * a + 3)
                rows = stack_dram[0, a, 0:J].rearrange("h (d i j) s -> (h d) i j s", i=PARTS, j=PARTS)
                for n in range(PARTS):
                    dst = rows[:, :, n, :] if a == 0 else rows[:, n, :, :]
                    sp.dma_start(dst, parts[0:R, 0, a]).then_inc(first_written, 16)
            sp.wait_ge(first_written, 2 * PARTS * 16)
            sp.wait_ge(stack_set, 2)
            load_slice(0, 0)
            for b in range(B):
                for a in range(2):
                    sp.wait_ge(prep_split, 3 * (2 * b + a) + 3)
                    h0 = J if b == 0 else 0
                    rows = stack_dram[b, a, h0:].rearrange("h (d i j) s -> (h d) i j s", i=PARTS, j=PARTS)
                    for n in range(PARTS):
                        dst = rows[:, :, n, :] if a == 0 else rows[:, n, :, :]
                        sp.dma_start(dst, parts[h0 * D:, b, a]).then_inc(parts_written[b], 16)
                if b == 0:
                    sp.wait_ge(parts_written[0], 2 * PARTS * 16)
                    for g in range(1, G):
                        load_slice(0, g)
                    sp.dma_start(gamma_sb[:], bass.AP(gamma.tensor, 0, [[0, P], [1, E]])).then_inc(rows_loaded, 16)
                    sp.dma_start(scale_sb[:], bass.AP(ffn_scale.tensor, 0, [[0, P], [1, 1]])).then_inc(rows_loaded, 16)
                if b == B - 2:
                    load_shift(0, 0)
            sp.dma_start(down_sb[:], values_down.rearrange("n d p -> d n p")).then_inc(experts_loaded, 16)
            sp.dma_start(up_sb[:], values_up.rearrange("(j n) p d -> (n p) j d", j=FJ)).then_inc(experts_loaded, 16)
            for b in range(1, B):
                sp.wait_ge(parts_written[b], 2 * PARTS * 16)

            def round_(t, attention, experts, more):
                if attention:
                    if not is0(t):
                        load_slice(t, G - 1)
                    load_shift(t, 1)
                    if more:
                        load_slice(t + 1, 0)
                    load_shift(t, 2)
                    if more:
                        load_slice(t + 1, 1)
                    load_shift(t, 3)
                if experts:
                    f = t - 1
                    sp.wait_ge(misc_done, job(t, "wt", is_kept))
                    apart(sp)
                    sp.dma_start(w_dram.rearrange("n c q -> c n q"), w_t[:, :]).then_inc(w_written, 16)
                    sp.wait_ge(w_written, f * 16 + 16)
                    for j in range(FJ):
                        src = bass.AP(w_dram.tensor, j * NJ * S, [[S, NJ], [0, PD], [1, S]])
                        sp.dma_start(w_rows[:, j, :], src).then_inc(w_loaded[j], 16)
                if attention and more:
                    load_slice(t + 1, 2)
                    load_shift(t + 1, 0)
                if experts:
                    sp.wait_ge(y_made, t)
                    apart(sp)
                    sp.dma_start(out[t - 1].rearrange("(c p) e -> p c e", p=P), y_out[:]).then_inc(y_stored, 16)

            rounds(sp, round_)
            sp.wait_ge(y_stored, 16 * B + 1)

        @block.gpsimd
        def _(pool):
            def split_shift(t, g):
                n, m = t * G + g, neg_max[:, g % 2, :]
                pool.wait_ge(max_ready, n * (J * C) + J * C)
                if not (is0(t) and g == 0):
                    pool.wait_ge(misc_ready, shift_job(t, g - 1, is_misc) if g else shift_job(t - 1, G - 1, is_misc))
                    apart(pool)
                nc.gpsimd.tensor_copy(shift_parts[:, 0, :], m).then_inc(shift_chain, 1)
                pool.wait_ge(shift_chain, n * 3 + 1)
                nc.gpsimd.tensor_sub(shift_res[:], m, shift_parts[:, 0, :]).then_inc(shift_chain, 1)
                pool.wait_ge(shift_chain, n * 3 + 2)
                apart(pool)
                nc.gpsimd.tensor_copy(shift_parts[:, 1, :], shift_res[:]).then_inc(shift_chain, 1)
                pool.wait_ge(shift_chain, n * 3 + 3)
                nc.gpsimd.tensor_sub(shift_parts[:, 2, :], shift_res[:], shift_parts[:, 1, :]).then_inc(shift_split, 1)

            def fetch_values(t, g):
                if not is0(t):
                    pool.wait_ge(pv_done, (t - 1) * U + C * (g + 1))
                    apart(pool)
                nc.gpsimd.tensor_copy(v_cur[:, :, g * J:(g + 1) * J, 0:D],
                                      v_all[:, :, g * J:(g + 1) * J, t, :]).then_inc(v_ready, 1)

            def norm(f, k, eps, dst, src, centre=True):
                pool.wait_ge(dve_step, dve_at(f, k + "mv"))
                apart(pool)
                nc.gpsimd.tensor_scalar(veps[:], mv[:, :, 1], eps, None, ALU.add).then_inc(pool_step, 1)
                if centre:
                    nc.gpsimd.tensor_tensor(dst, src, mv[:, :, 0:1].to_broadcast([P, C, E]), ALU.subtract) \
                        .then_inc(pool_step, 1)
                pool.wait_ge(pool_step, pool_at(f, k + "eps"))
                nc.gpsimd.tensor_tensor(rstd[:], veps[:], minus_half[:], ALU.pow).then_inc(pool_step, 1)
                if centre:
                    pool.wait_ge(pool_step, pool_at(f, k + "pow"))
                    return nc.gpsimd.tensor_tensor(dst, dst, rstd[:].unsqueeze(2).to_broadcast([P, C, E]), ALU.mult)

            def weigh(f, t, j):
                pool.wait_ge(hidden_made, hidden_count(f, j))
                pool.wait_ge(w_loaded[j], f * 16 + 16)
                nc.gpsimd.tensor_tensor(hid[:, j], hid[:, j], w_rows[:, j], ALU.mult).then_inc(weighed, 1)

            nc.gpsimd.memset(ident[:], 0.0).then_inc(consts_made, 1)
            pool.wait_ge(consts_made, 1)
            nc.gpsimd.affine_select(out=ident[:], in_=ident[:], compare_op=ALU.not_equal, fill=1.0, base=0,
                                    pattern=[[-1, P]], channel_multiplier=1).then_inc(consts_made, 1)
            two_ones = 1.0019378662109375
            pool.wait_ge(consts_made, 2)
            nc.gpsimd.memset(k_stack[64:P].bitcast(F32), two_ones).then_inc(stack_set, 1)
            pool.wait_ge(stack_set, 1)
            nc.gpsimd.memset(q_stack[64:P].bitcast(F32), 0.0).then_inc(stack_set, 1)
            pool.wait_ge(stack_set, 2)
            nc.gpsimd.memset(v_cur[:], 0.0).then_inc(consts_made, 1)
            nc.gpsimd.memset(minus_half[:], -0.5).then_inc(consts_made, 1)
            nc.gpsimd.memset(zeros[:], 0.0).then_inc(consts_made, 1)
            nc.gpsimd.memset(shift_parts[:], 0.0).then_inc(consts_made, 1)
            pool.wait_ge(consts_made, 6)
            nc.gpsimd.tensor_copy(ident_bf[:], ident[:]).then_inc(consts_made, 1)
            nc.gpsimd.memset(v_cur[:, :, :, D:D + 1], 1.0).then_inc(consts_made, 1)
            pool.wait_ge(consts_made, 8)
            pool.wait_ge(beta_loaded, 16)
            for b in range(B):
                pool.wait_ge(prep_mm, 4 * b + 1)
                nc.gpsimd.tensor_tensor(x_sb[:, b], x_sb[:, b], beta_sb[:].unsqueeze(1).to_broadcast([P, C, E]),
                                        ALU.add).then_inc(xb_ready, 1)
            for g in range(G):
                fetch_values(0, g)
            split_shift(0, 0)

            def round_(t, attention, experts, more):
                f = t - 1
                if attention and not is0(t):
                    fetch_values(t, G - 1)
                if experts:
                    pool.wait_ge(side_done, job(t, "o3", is_side))
                    nc.gpsimd.tensor_tensor(z[:].rearrange("p c (h d) -> p c h d", d=D),
                                            attn[:].rearrange("p c (h d) -> p c h d", d=D),
                                            bias_v[:, :, :, f, :], ALU.add).then_inc(pool_step, 1)
                if attention:
                    split_shift(t, 1)
                if experts:
                    norm(f, "a", EPS_ATTENTION, z[:], z[:]).then_inc(pool_step, 1)
                    pool.wait_ge(pool_step, pool_at(f, "ascale"))
                    nc.gpsimd.tensor_tensor(z[:], z[:], gamma_sb[:].unsqueeze(1).to_broadcast([P, C, E]),
                                            ALU.mult).then_inc(pool_step, 1)
                    pool.wait_ge(pool_step, pool_at(f, "gamma"))
                    nc.gpsimd.tensor_tensor(z[:], z[:], x_sb[:, f], ALU.add).then_inc(pool_step, 1)
                    norm(f, "b", EPS_LN, x1[:], z[:]).then_inc(pool_step, 1)
                if attention:
                    if more:
                        fetch_values(t + 1, 0)
                    split_shift(t, 2)
                if experts:
                    pool.wait_ge(dve_step, dve_at(f, "top"))
                    nc.gpsimd.tensor_tensor(sdiff[:], sim[:], top[:, :, 0:1].to_broadcast([P, C, NE]),
                                            ALU.subtract).then_inc(pool_step, 1)
                if attention:
                    if more:
                        fetch_values(t + 1, 1)
                    split_shift(t, 3)
                if experts:
                    for j in range(FJ - 2) if attention else TAIL_POOL:
                        weigh(f, t, j)
                if attention and more:
                    fetch_values(t + 1, 2)
                if experts and attention:
                    weigh(f, t, FJ - 2)
                if attention and more:
                    split_shift(t + 1, 0)
                if experts and attention:
                    weigh(f, t, FJ - 1)
                    pool.wait_ge(y_stored, f * 16 + 1)
                    norm(f, "c", EPS_LN, y_out[:], y[:]).then_inc(y_made, 1)
                elif experts:
                    norm(f, "c", EPS_LN, None, None, centre=False)

            rounds(pool, round_)

        @block.scalar
        def _(act):
            def copy(dst, src, scale=1.0):
                return nc.scalar.activation(dst, src, ACT.Copy, scale=scale)

            for b in range(B):
                turned, q_made, k_made = prep_banks(b)
                act.wait_ge(prep_mm, 4 * b + 1)
                copy(x_t[:, b % 2, :], turned).then_inc(prep_copied, 1)
                for a, made in enumerate((q_made, k_made)):
                    act.wait_ge(prep_mm, 4 * b + 2 + a)
                    copy(parts[:, b, a, 0, :], made).then_inc(prep_copied, 1)
                act.wait_ge(prep_mm, 4 * b + 4)
                copy(v_all[:, :, :, b, :].rearrange("p c h d -> p (c h) d"),
                     turned.rearrange("p (n d) -> p n d", d=D)).then_inc(prep_copied, 1)
            act.wait_ge(table_mm, 1)
            copy(rel_t[:], st_ps[:, 0, :]).then_inc(table_copied, 1)
            act.wait_ge(table_mm, 2)
            copy(keys_t[:], st_ps[0:PD, 1, 0:NE]).then_inc(table_copied, 1)
            act.wait_ge(table_mm, 3)
            copy(sim_w[:], st_ps[:, 2, 0:NE]).then_inc(table_copied, 1)

            def bias_copy(g):
                act.wait_ge(bias_mm, g - CG + 2)
                if g >= CG + 2:
                    act.wait_ge(bias_turned, g - CG - 1)
                n = constant_from((g + 1) * J - 1) + 1
                turned = bias_t[:, g % 2, :].rearrange("p (a r) -> p r a", r=H)
                made = bias_banks(g)[0][:, 0:n * HPB].rearrange("p (r a) -> p r a", r=n)
                copy(turned[:, 0:n, :], made)
                copy(turned[:, n:, :], made[:, n - 1:n, :].to_broadcast([P, H - n, HPB])).then_inc(bias_copied, 1)

            def bias_keep(g):
                act.wait_ge(bias_turned, g - CG + 1)
                copy(bias_v[:, :, g * J:(g + 1) * J].rearrange("p c j b d -> p c (j b d)"),
                     bias_banks(g)[1].rearrange("p (c n) -> p c n", c=C)).then_inc(bias_kept, 1)

            def bias_spread():
                act.wait_ge(bias_mm, 1)
                n = CG * J * B * D
                copy(bias_v[:, :, 0:CG * J].rearrange("p c h b d -> p c (h b d)"),
                     st_ps[:, 2, 0:n].unsqueeze(1).to_broadcast([P, C, n])).then_inc(bias_kept, 1)

            def shift_copy(t, g):
                act.wait_ge(misc_ready, shift_job(t, g, is_misc))
                if not (is0(t) and g == 0):
                    act.wait_ge(shift_loaded[(g - 1) % G], 16 * (t if g == 0 else t + 1))
                copy(shift_rows[:, :], mi_bf[0:PARTS * J * C, 0:P]).then_inc(misc_done, 1)

            mi_bf = mi_ps[:, :].bitcast(BF16)
            bias_spread()
            for g in range(CG, G):
                bias_copy(g)
                if g > CG:
                    bias_keep(g - 1)
            bias_keep(G - 1)
            shift_copy(0, 0)
            act.wait_ge(rows_loaded, 32)
            copy(half_scale[:], scale_sb[:], 0.5).then_inc(table_copied, 1)

            def exp(t, u, j):
                n = t * U + u
                act.wait_ge(scores_ready, J * n + j + 1)
                if j == 0 and not (is0(t) and u < 2):
                    act.wait_ge(pv_done, n - 1)
                nc.scalar.activation(probs[:, u % 2, j, :], st_ps[:, score_bank(u * J + j), :], ACT.Exp,
                                     scale=SCORE_SCALE).then_inc(probs_ready, 1)

            def o_copy(t, g):
                act.wait_ge(pv_done, t * U + C * (g + 1))
                if not (is0(t) and g == 0):
                    name = f"o{(g - 1) % G}"
                    act.wait_ge(*((side_ready, job(t, name, is_side)) if is_side(name) else
                                  (misc_ready, job(t, name, is_misc))))
                copy(o_sb[:], ov_ps[:]).then_inc(o_copied, 1)

            def expert_copy(t, name):
                f = t - 1
                if name == "x1t":
                    act.wait_ge(side_ready, job(t, name, is_side))
                    copy(x1_t[:], si_ps[:]).then_inc(side_done, 1)
                    return
                if name == "sim":
                    act.wait_ge(side_ready, job(t, name, is_side))
                    copy(sim[:].rearrange("p c n -> p (c n)"), si_ps[:, 0:C * NE]).then_inc(side_done, 1)
                    return
                act.wait_ge(misc_ready, job(t, name, is_misc))
                if name == "wt":
                    copy(w_t[:], mi_ps[:, 0:P]).then_inc(misc_done, 1)
                else:
                    j = int(name[4:])
                    nc.scalar.activation(tanh_sb[:, j % 3, :], down_bank(t, j), ACT.Tanh, scale=0.5).then_inc(act_step, 1)

            def round_(t, attention, experts, more):
                def copies(half):
                    for name in half:
                        if name.startswith("shift") and here(name, attention, experts, more):
                            shift_copy(*((t, int(name[5:])) if name != "shift0" else (t + 1, 0)))
                        elif name in ("x1t", "sim", "wt") or name.startswith("down"):
                            if experts:
                                expert_copy(t, name)

                for u in range(U):
                    before, behind = JOBS.get(u, ([], []))
                    if attention:
                        for j in range(J - 1):
                            exp(t, u, j)
                    if u == 0 and experts:
                        o_copy(t - 1, G - 1)
                    if u and u % C == 0 and attention:
                        o_copy(t, u // C - 1)
                    copies(before)
                    if u == 7 and experts:
                        act.wait_ge(pool_step, pool_at(t - 1, "sdiff"))
                        nc.scalar.activation(sexp[:], sdiff[:], ACT.Exp).then_inc(act_step, 1)
                    if attention:
                        exp(t, u, J - 1)
                    copies(behind)

            rounds(act, round_)

        @block.vector
        def _(dve):
            def split(b):
                for a in range(2):
                    n = 3 * (2 * b + a)
                    hi, mid, lo = (parts[:, b, a, i, :] for i in range(PARTS))
                    dve.wait_ge(prep_copied, 4 * b + 2 + a)
                    nc.vector.tensor_sub(resid[:, a], prep_banks(b)[1 + a], hi).then_inc(prep_split, 1)
                    dve.wait_ge(prep_split, n + 1)
                    nc.vector.tensor_copy(mid, resid[:, a]).then_inc(prep_split, 1)
                    dve.wait_ge(prep_split, n + 2)
                    nc.vector.tensor_sub(lo, resid[:, a], mid).then_inc(prep_split, 1)

            for b in range(B - 1):
                split(b)

            def maximum(t, pos, c):
                n, g = t * U + pos, (pos // J) % G
                dve.wait_ge(sm_ready, C * n + c + 1)
                if pos % J == 0 and c == 0 and not (is0(t) and pos // J < 2):
                    dve.wait_ge(shift_split, t * G + pos // J - 1)
                col = (pos % J) * C + c
                nc.vector.tensor_reduce(neg_max[:, g % 2, col:col + 1], sm_ps[:, c % 2, :], AX.X, ALU.max,
                                        negate=True).then_inc(max_ready, 1)

            for pos in range(LEAD):
                if pos == J:
                    split(B - 1)
                for c in range(C):
                    maximum(0, pos, c)

            def attend(t, g, in_round):
                name = f"o{g}"
                if is_side(name):
                    dve.wait_ge(side_ready, job(in_round, name, is_side))
                else:
                    dve.wait_ge(misc_ready, job(in_round, name, is_misc))
                bank, done = (si_ps, side_done) if is_side(name) else (mi_ps, misc_done)
                o = bank[:].rearrange("p (c j w) -> p c j w", c=C, j=J)
                n = t * G + g
                nc.vector.reciprocal(rsum[:], o[:, :, :, D]).then_inc(rsum_ready, 1)
                dve.wait_ge(rsum_ready, n + 1)
                nc.vector.tensor_tensor(attn[:, :, g * J * D:(g + 1) * J * D].rearrange("p c (j d) -> p c j d", d=D),
                                        o[:, :, :, 0:D], rsum[:].unsqueeze(3).to_broadcast([P, C, J, D]),
                                        ALU.mult).then_inc(done, 1)

            def stats_of(f, k, src):
                for c in range(C):
                    i = nc.vector.bn_stats(stats[:, c, :], src[:, c, :])
                i.then_inc(dve_step, 1)

            def mv_of(f, k):
                dve.wait_ge(dve_step, dve_at(f, k + "stats"))
                apart(dve)
                for c in range(C):
                    i = nc.vector.bn_aggr(mv[:, c, :], stats[:, c, :])
                i.then_inc(dve_step, 1)

            def after(f, name):
                dve.wait_ge(dve_step, dve_at(f, name))

            def step(i):
                i.then_inc(dve_step, 1)

            def flat(a):
                return a[:].rearrange("p c n -> p (c n)")

            def hidden(t, j):
                dve.wait_ge(act_step, act_at(t - 1, f"tanh{j}"))
                nc.vector.scalar_tensor_tensor(out=hid[:, j], in0=tanh_sb[:, j % 3, :], scalar=1.0, in1=down_bank(t, j),
                                               op0=ALU.add, op1=ALU.mult).then_inc(hidden_made, 1)

            def expert_steps(t, u, s, attention):
                f = t - 1
                at = (u, s)
                if at == (1, 0):
                    attend(f, G - 1, t)
                elif at == (1, 3):
                    dve.wait_ge(pool_step, pool_at(f, "bias"))
                    stats_of(f, "a", z)
                elif at == (2, 0):
                    mv_of(f, "a")
                elif at == (4, 1):
                    dve.wait_ge(pool_step, pool_at(f, "resid"))
                    stats_of(f, "b", z)
                elif at == (4, 2):
                    mv_of(f, "b")
                elif at == (6, 3):
                    dve.wait_ge(side_done, job(t, "sim", is_side))
                    apart(dve)
                    for c in range(C):
                        i = nc.vector.max(top[:, c, :], sim[:, c, :])
                    step(i)
                elif at == (7, 1):
                    after(f, "top")
                    fourth = top[:, :, TOPK - 1:TOPK].to_broadcast([P, C, NE])
                    step(nc.vector.tensor_tensor(above[:], sim[:], fourth, ALU.is_gt))
                    step(nc.vector.tensor_tensor(ties[:], sim[:], fourth, ALU.is_equal))
                elif at == (7, 2):
                    after(f, "above")
                    step(nc.vector.tensor_reduce(n_above[:], above[:], AX.X, ALU.add))
                elif at == (7, 3):
                    after(f, "n_above")
                    for c in range(C):
                        i = nc.vector.tensor_tensor_scan(rank[:, c, :], ties[:, c, :], zeros[:], n_above[:, c:c + 1],
                                                         ALU.add, ALU.add)
                    step(i)
                elif at == (8, 1):
                    after(f, "rank")
                    step(nc.vector.scalar_tensor_tensor(out=flat(keep), in0=flat(rank), scalar=float(TOPK),
                                                        in1=flat(ties), op0=ALU.is_le, op1=ALU.mult))
                elif at == (8, 2):
                    after(f, "keep")
                    step(nc.vector.tensor_tensor(mask[:], keep[:], above[:], ALU.add))
                    after(f, "mask")
                    dve.wait_ge(act_step, act_at(f, "sexp"))
                    step(nc.vector.tensor_tensor(wexp[:], sexp[:], mask[:], ALU.mult))
                elif at == (8, 3):
                    after(f, "wexp")
                    step(nc.vector.tensor_reduce(wsum[:], wexp[:], AX.X, ALU.add))
                    after(f, "wsum")
                    step(nc.vector.reciprocal(winv[:], wsum[:]))
                elif at == (9, 1):
                    after(f, "winv")
                    step(nc.vector.tensor_scalar(wscale[:], winv[:], half_scale[:, 0:1], None, ALU.mult))
                    after(f, "wscale")
                    step(nc.vector.tensor_tensor(w_tok[:], wexp[:], wscale[:].unsqueeze(2).to_broadcast([P, C, NE]),
                                                 ALU.mult))
                elif at == (14, 3) and not attention:
                    for j in TAIL_VECTOR:
                        dve.wait_ge(hidden_made, hidden_count(f, j))
                        dve.wait_ge(w_loaded[j], f * 16 + 16)
                        nc.vector.tensor_tensor(hid[:, j], hid[:, j], w_rows[:, j], ALU.mult).then_inc(tail_weighed, 1)
                elif at == (15, 0):
                    dve.wait_ge(side_ready, job(t, f"up{FJ - 1}", is_side))
                    nc.vector.scalar_tensor_tensor(out=flat(y), in0=flat(x1), scalar=2.0, in1=si_ps[:],
                                                   op0=ALU.mult, op1=ALU.add).then_inc(side_done, 1)
                elif at == (15, 1):
                    dve.wait_ge(side_done, job(t, f"up{FJ - 1}", is_side))
                    stats_of(f, "c", y)
                elif at == (15, 2):
                    mv_of(f, "c")
                    if not attention:
                        dve.wait_ge(pool_step, pool_at(f, "cpow") - 1)
                        dve.wait_ge(y_stored, f * 16 + 1)
                        for c in range(C):
                            i = nc.vector.tensor_scalar(y_out[:, c, :], y[:, c, :], mv[:, c, 0:1], rstd[:, c:c + 1],
                                                        ALU.subtract, ALU.mult)
                        i.then_inc(y_made, 1)
                if s == 0 and 7 <= u < 7 + FJ:
                    hidden(t, u - 7)

            def round_(t, attention, experts, more):
                for u in range(U):
                    for s in range(C):
                        if attention and (more or u + LEAD < U):
                            maximum(t, u + LEAD, s)
                        if attention and s == 0 and u in (5, 9, 15):
                            g = {5: 0, 9: 1, 15: 2}[u]
                            attend(t, g, t)
                        if experts:
                            expert_steps(t, u, s, attention)

            rounds(dve, round_)

        @block.tensor
        def _(pe):
            mi_bf = mi_ps[:, :].bitcast(BF16)
            pitch = rel_t[:, :].ap[0][0]

            def prep(b):
                if b == 0:
                    pe.wait_ge(consts_made, 2)
                pe.wait_ge(x_loaded[b], 16)
                if b >= 2:
                    pe.wait_ge(prep_copied, 4 * (b - 2) + 4)
                    pe.wait_ge(prep_split, 3 * (2 * (b - 2) + 1) + 1)
                turned, q_made, k_made = prep_banks(b)
                for c in range(C):
                    i = nc.tensor.transpose(turned[:, c * P:(c + 1) * P], x_sb[:, b, c, :], ident[:])
                i.then_inc(prep_mm, 1)
                if b == 0:
                    pe.wait_ge(proj_loaded, 48)
                pe.wait_ge(prep_copied, 4 * b + 1)
                xt = x_t[:, b % 2, :]
                nc.tensor.matmul(q_made, wq_sb[:], xt, start=True, stop=True).then_inc(prep_mm, 1)
                nc.tensor.matmul(k_made, wk_sb[:], xt, start=True, stop=True).then_inc(prep_mm, 1)
                for c in range(C):
                    i = nc.tensor.matmul(turned[:, c * P:(c + 1) * P], xt[:, c * P:(c + 1) * P],
                                         wv_sb[:], start=True, stop=True)
                i.then_inc(prep_mm, 1)

            def maximum_scores(t, pos, c):
                n, h = t * U + pos, pos % U
                k = C * n + c
                if pos % J == 0 and c == 0:
                    pe.wait_ge(stack_loaded[pos // J % G], 32 * (t + pos // U) + 32)
                if not (is0(t) and pos == 0 and c < 2):
                    pe.wait_ge(max_ready, k - 1)
                nc.tensor.matmul(sm_ps[:, c % 2, :], q_stack[0:SHIFT_ROW, h, c * P:(c + 1) * P],
                                 k_stack[0:SHIFT_ROW, h, :], start=True, stop=True).then_inc(sm_ready, 1)

            def scores(t, u, j):
                n, g, kc, k = t * U + u, u // C, u % C, u * J + j
                if j == 0 and kc == 0:
                    pe.wait_ge(shift_loaded[g], 16 * t + 16)
                if not (is0(t) and k < 3):
                    pe.wait_ge(probs_ready, J * n + j + 1 - scores_since(k))
                nc.tensor.matmul(st_ps[:, score_bank(k), :], k_stack[:, g * J + j, kc * P:(kc + 1) * P],
                                 q_stack[:, g * J + j, :], start=True, stop=True).then_inc(scores_ready, 1)

            def values(t, u):
                n, g, kc = t * U + u, u // C, u % C
                if kc == 0:
                    pe.wait_ge(v_ready, t * G + g + 1)
                    if not (is0(t) and g == 0):
                        pe.wait_ge(o_copied, t * G + g)
                pe.wait_ge(probs_ready, J * n + J)
                for j in range(J):
                    i = nc.tensor.matmul(ov_ps[j * TILE:(j + 1) * TILE, :], v_cur[:, kc, g * J + j, :],
                                         probs[:, u % 2, j, :], start=(kc == 0), stop=(kc == C - 1))
                i.then_inc(pv_done, 1)

            def turn(dst, src, idn):
                return nc.tensor.transpose(dst, src, idn)

            def up(f, j, tail):
                if tail and j in TAIL_VECTOR:
                    pe.wait_ge(tail_weighed, TAIL_VECTOR.index(j) + 1)
                elif tail:
                    pe.wait_ge(weighed, f * FJ + TAIL_POOL.index(j) + 1)
                else:
                    pe.wait_ge(weighed, hidden_count(f, j))
                for c in range(C):
                    i = nc.tensor.matmul(si_ps[:, c * P:(c + 1) * P], hid[:, j, c * P:(c + 1) * P], up_sb[:, j, :],
                                         start=(j == 0 and c == 0), stop=(j == FJ - 1), skip_group_check=True)
                if j == FJ - 1:
                    i.then_inc(side_ready, 1)

            def misc(t, name, kind):
                f = t - 1
                if name.startswith("up"):
                    j = int(name[2:])
                    if j == 0:
                        pe.wait_ge(side_done, job(t, f"up{FJ - 1}", is_side) - 1)
                    up(f, j, not kind[0])
                    return
                bank, ready = (si_ps, side_ready) if is_side(name) else (mi_ps, misc_ready)
                if is_side(name):
                    pe.wait_ge(side_done, job(t, name, is_side) - 1)
                elif not (name.startswith("down") and down_bank(t, 0) is not mi_ps and isinstance(t, int) and t == B):
                    count = job(t, name, is_kept)
                    pe.wait_ge(misc_done, count - 1 if is_kept(name) else count)
                    names = [n for u in sorted(JOBS) for half in JOBS[u] for n in half
                             if is_misc(n) and here(n, *kind)]
                    last = names[names.index(name) - 1] if names[0] != name else name
                    if last != name and last.startswith("down"):
                        pe.wait_ge(hidden_made, hidden_count(f, int(last[4:])))
                elif int(name[4:]) >= 3:
                    pe.wait_ge(hidden_made, hidden_count(f, int(name[4:]) - 3))
                if name.startswith("o"):
                    g = int(name[1:])
                    pe.wait_ge(o_copied, (f if g == G - 1 else t) * G + g + 1)
                    for c in range(C):
                        i = turn(bank[:, c * P:(c + 1) * P], o_sb[:, c * P:(c + 1) * P], ident[:])
                elif name.startswith("shift"):
                    g = int(name[5:])
                    pe.wait_ge(shift_split, (t + 1 if g == 0 else t) * G + g + 1)
                    i = turn(mi_bf[:, 0:P], shift_parts[:].rearrange("p i n -> p (i n)"), ident_bf[:])
                elif name == "x1t":
                    pe.wait_ge(pool_step, pool_at(f, "bscale"))
                    for c in range(C):
                        i = turn(bank[:, c * P:(c + 1) * P], x1[:, c, :], ident[:])
                elif name == "sim":
                    pe.wait_ge(side_done, job(t, "x1t", is_side))
                    for c in range(C):
                        i = nc.tensor.matmul(bank[:, c * NE:(c + 1) * NE], x1_t[:, c * P:(c + 1) * P], sim_w[:],
                                             start=True, stop=True)
                elif name == "wt":
                    pe.wait_ge(dve_step, dve_at(f, "w"))
                    i = turn(bank[:, 0:P], w_tok[:].rearrange("p c n -> p (c n)"), ident[:])
                else:
                    j = int(name[4:])
                    if j == 0:
                        pe.wait_ge(experts_loaded, 32)
                    i = nc.tensor.matmul(down_bank(t, j), down_sb[:, j * NJ:(j + 1) * NJ, :], x1_t[:],
                                         start=True, stop=True)
                i.then_inc(ready, 1)

            early = [(pos, c) for pos in range(LEAD) for c in range(C)]

            def early_maxima(n):
                for _ in range(n):
                    if early:
                        maximum_scores(0, *early.pop(0))

            for b in range(B):
                prep(b)
            early_maxima(3)
            pe.wait_ge(rel_loaded, 16)
            pe.wait_ge(prep_copied, 4 * (B - 1) + 4)
            pe.wait_ge(prep_split, 3 * (2 * (B - 2) + 1) + 1)
            for n in range(NWIN // P):
                i = turn(st_ps[:, 0, n * P:(n + 1) * P], rel_win[:, n, :], ident[:])
            i.then_inc(table_mm, 1)
            pe.wait_ge(keys_loaded, 32)
            early_maxima(1)
            turn(st_ps[0:PD, 1, 0:NE], keys_sb[:], ident[0:NE, 0:NE]).then_inc(table_mm, 1)
            early_maxima(1)
            pe.wait_ge(table_copied, 2)
            nc.tensor.matmul(st_ps[:, 2, 0:NE], hasher_sb[:], keys_t[:], start=True, stop=True).then_inc(table_mm, 1)

            pe.wait_ge(table_copied, 3)
            for kc in range(C):
                i = nc.tensor.matmul(st_ps[:, 2, 0:CG * J * B * D], rel_t[:, LAST:LAST + P],
                                     v_all[:, kc, 0:CG * J].rearrange("p h b d -> p (h b d)"),
                                     start=(kc == 0), stop=(kc == C - 1))
                early_maxima(1 + kc % 2)
            i.then_inc(bias_mm, 1)

            def bias_turn(g):
                pe.wait_ge(bias_copied, g - CG + 1)
                pe.wait_ge(bias_kept, g - CG + 1) if g == CG else pe.wait_ge(bias_copied, 2)
                for c in range(C):
                    i = turn(bias_banks(g)[1][:, c * P:(c + 1) * P], bias_t[:, g % 2, c * P:(c + 1) * P], ident[:])
                i.then_inc(bias_turned, 1)

            for g in range(CG, G):
                if g >= CG + 2:
                    pe.wait_ge(bias_copied, g - CG - 1)
                n = constant_from((g + 1) * J - 1) + 1
                for kc in range(C):
                    for j in range(J):
                        h = g * J + j
                        window = bass.AP(rel_t, S - 1 - HPB * h + (P // H) * kc, [[pitch, P], [HPB, n], [-1, HPB]])
                        i = nc.tensor.matmul(bias_banks(g)[0][j * TILE:(j + 1) * TILE, 0:n * HPB], v_all[:, kc, h].rearrange("p b d -> p (b d)"),
                                             window, start=(kc == 0), stop=(kc == C - 1))
                    if kc == C - 1:
                        i.then_inc(bias_mm, 1)
                    early_maxima(1)
                if g > CG:
                    bias_turn(g - 1)
            bias_turn(G - 1)
            early_maxima(J * C + 2 - (LEAD * C - len(early)))
            pe.wait_ge(prep_split, 3 * (2 * B - 2) + 1)
            pe.wait_ge(consts_made, 8)
            pe.wait_ge(shift_split, 1)
            turn(mi_bf[:, 0:P], shift_parts[:].rearrange("p i n -> p (i n)"), ident_bf[:]) \
                .then_inc(misc_ready, 1)
            early_maxima(len(early))
            pe.wait_ge(bias_kept, G - CG + 1)
            pe.wait_ge(prep_split, 3 * (2 * B - 1) + 1)

            def round_(t, attention, experts, more):
                def jobs(half):
                    for name in half:
                        if here(name, attention, experts, more) and (attention or name[:2] != "up"):
                            misc(t, name, (attention, experts, more))

                for u in range(U):
                    before, behind = JOBS.get(u, ([], []))

                    def maxima(c):
                        if attention and (more or u + LEAD < U):
                            maximum_scores(t, u + LEAD, c)

                    def score(*heads):
                        for j in heads:
                            if attention:
                                scores(t, u, j)
                    score(0)
                    maxima(0)
                    score(1, 2)
                    maxima(1)
                    if u and attention:
                        values(t, u - 1)
                    elif u == 0 and experts:
                        values(t - 1, U - 1)
                    maxima(2)
                    jobs(before)
                    score(3)
                    maxima(3)
                    jobs(behind)
                if not attention:
                    for j in range(FJ):
                        misc(t, f"up{j}", (attention, experts, more))

            rounds(pe, round_)


_INS = ["L0_attn_x", "L0_attn_Wq", "L0_attn_Wk", "L0_attn_Wv", "L0_attn_rel_table", "L0_attn_gamma", "L0_attn_beta",
        "L0_ffn_hasher_w", "L0_ffn_keys", "L0_ffn_values_down", "L0_ffn_values_up", "L0_ffn_scale"]


def kernel(**inputs):
    import numpy as np
    import concourse.bacc as bacc
    from concourse import mybir as _mybir
    from concourse.bass_utils import run_bass_kernel_spmd

    nc = bacc.Bacc("TRN2", target_bir_lowering=False, num_devices=1)
    arrays, args = {}, []
    for name in _INS:
        a = np.ascontiguousarray(inputs[name])
        arrays[name] = a
        args.append(nc.dram_tensor(name, a.shape, _mybir.dt.from_np(a.dtype), kind="ExternalInput").ap())
    shape = arrays["L0_attn_x"].shape
    args.append(nc.dram_tensor("out", shape, _mybir.dt.float32, kind="ExternalOutput").ap())
    bass_postln_attention_product_key_ffn(nc, *args)
    return run_bass_kernel_spmd(nc, [arrays], core_ids=[0]).results[0]["out"]
```

```python
import concourse.bass as bass
from concourse import mybir
from contextlib import ExitStack


def bass_postln_attention_product_key_ffn(nc, x, w_q, w_k, w_v, rel_table, gamma, beta,
                                          hasher_w, keys, values_down, values_up, ffn_scale, out):
    F32, BF16 = mybir.dt.float32, mybir.dt.bfloat16
    ALU, ACT, AX = mybir.AluOpType, mybir.ActivationFunctionType, mybir.AxisListType

    B, S, E = x.shape
    H = rel_table.shape[1]
    D = E // H
    P = 128
    C = S // P
    J = 4
    G = H // J
    U = G * C
    NE, PD = keys.shape
    NJ = P // PD
    FJ = NE // NJ
    TOPK = 4
    PARTS = 3
    TERMS = PARTS * PARTS * D
    SHIFT_ROW = 96
    SCORE_SCALE = float(E) ** -0.5
    LEAD = 7
    EARLY = LEAD * C
    HPB = S // H
    LAST = rel_table.shape[0] - 1
    NWIN = S
    TILE = 32
    EPS_ATTENTION, EPS_LN = 1e-3, 1e-5

    def constant_from(h):
        return min(max(-(-(LAST - S + HPB + HPB * h) // HPB), 0), H)

    CG = sum(constant_from((g + 1) * J - 1) == 0 for g in range(G))
    assert B % 2 == 0 and CG == G - 2
    assert all(S - 1 - HPB * g * J + (C - 1) * P // H + HPB * constant_from((g + 1) * J - 1) < NWIN
               for g in range(CG, G)) and NWIN - P >= LAST and constant_from(H - 1) < H

    ctx = ExitStack()
    with ctx:
        def sb(name, shape, dt=F32):
            return ctx.enter_context(nc.sbuf_tensor(name, shape, dt))

        def pb(name, shape, dt=F32):
            return ctx.enter_context(nc.psum_tensor(name, shape, dt))

        def sem(name):
            return ctx.enter_context(nc.semaphore(name))

        ident, ident_bf = sb("ident", [P, P]), sb("ident_bf", [P, P], BF16)
        minus_half, zeros = sb("minus_half", [P, C]), sb("zeros", [P, NE])
        wq_sb, wk_sb, wv_sb = sb("wq_sb", [P, E]), sb("wk_sb", [P, E]), sb("wv_sb", [P, E])
        gamma_sb, beta_sb = sb("gamma_sb", [P, E]), sb("beta_sb", [P, E])
        hasher_sb, keys_sb, keys_t = sb("hasher_sb", [PD, E]), sb("keys_sb", [NE, PD]), sb("keys_t", [PD, NE])
        sim_w = sb("sim_w", [P, NE])
        down_sb = sb("down_sb", [P, NE, PD])
        up_sb = sb("up_sb", [P, FJ, E])
        scale_sb, half_scale = sb("scale_sb", [P, 1]), sb("half_scale", [P, 1])
        rel_win = sb("rel_win", [P, NWIN // P, P])
        rel_t = sb("rel_t", [P, NWIN])
        x_sb = sb("x_sb", [P, B, C, E])
        x_t = sb("x_t", [P, 2, S])
        parts = sb("parts", [P, B, 2, PARTS, S], BF16)
        resid = sb("resid", [P, 2, 2, S])
        v_all = sb("v_all", [P, C, H, B, D])
        v_cur = sb("v_cur", [P, C, H, TILE])
        q_stack, k_stack = sb("q_stack", [P, H, S], BF16), sb("k_stack", [P, H, S], BF16)
        neg_max = sb("neg_max", [P, 2, J * C])
        shift_parts = sb("shift_parts", [P, P // (J * C), J * C], BF16)
        shift_res = sb("shift_res", [P, J * C])
        shift_rows = sb("shift_rows", [PARTS * J * C, P], BF16)
        probs = sb("probs", [P, 2, J, S])
        o_sb = sb("o_sb", [P, S])
        rsum = sb("rsum", [P, C, J])
        attn = sb("attn", [P, C, E])
        bias_t = sb("bias_t", [P, 2, S])
        bias_v = sb("bias_v", [P, C, H, B, D])
        z = sb("z", [P, C, E])
        stats, mv = sb("stats", [P, C, 6]), sb("mv", [P, C, 2])
        late_stats, late_mv = sb("late_stats", [P, C, 6]), sb("late_mv", [P, C, 2])
        late_veps, late_rstd = sb("late_veps", [P, C]), sb("late_rstd", [P, C])
        veps, rstd = sb("veps", [P, C]), sb("rstd", [P, C])
        x1, x1_t = sb("x1", [P, C, E]), sb("x1_t", [P, S])
        sim, top = sb("sim", [P, C, NE]), sb("top", [P, C, 8])
        sdiff, sexp = sb("sdiff", [P, C, NE]), sb("sexp", [P, C, NE])
        above, ties, rank = sb("above", [P, C, NE]), sb("ties", [P, C, NE]), sb("rank", [P, C, NE])
        keep, mask, wexp = sb("keep", [P, C, NE]), sb("mask", [P, C, NE]), sb("wexp", [P, C, NE])
        n_above, wsum, winv, wscale = sb("n_above", [P, C]), sb("wsum", [P, C]), sb("winv", [P, C]), sb("wscale", [P, C])
        w_tok, w_t = sb("w_tok", [P, C, NE]), sb("w_t", [P, P])
        w_rows = sb("w_rows", [P, FJ, S])
        tanh_sb = sb("tanh_sb", [P, 3, S])
        hid = sb("hid", [P, FJ, S])
        y, y_out = sb("y", [P, C, E]), sb("y_out", [P, C, E])

        st_ps = pb("st_ps", [P, 3, S])
        sm_ps = pb("sm_ps", [P, 2, S])
        ov_ps = pb("ov_ps", [P, S])
        mi_ps = pb("mi_ps", [P, S])
        si_ps = pb("si_ps", [P, S])

        stack_dram = nc.dram_tensor("stack_dram", [B, 2, H, D * PARTS * PARTS, S], BF16, kind="Internal").ap()
        rel_dram = nc.dram_tensor("rel_dram", [NWIN + P // H, H], F32, kind="Internal").ap()
        w_dram = nc.dram_tensor("w_dram", [NE, C, P], F32, kind="Internal").ap()

        waits_met = sem("waits_met")
        consts_made, stack_set = sem("consts_made"), sem("stack_set")
        x_loaded = [sem(f"x_loaded{b}") for b in range(B)]
        proj_loaded, rows_loaded, beta_loaded = sem("proj_loaded"), sem("rows_loaded"), sem("beta_loaded")
        rel_written, rel_loaded = sem("rel_written"), sem("rel_loaded")
        keys_loaded, experts_loaded = sem("keys_loaded"), sem("experts_loaded")
        prep_mm, prep_copied, resid_made = sem("prep_mm"), sem("prep_copied"), sem("resid_made")
        first_split, mid_made, low_made = sem("first_split"), sem("mid_made"), sem("low_made")
        first_written = sem("first_written")
        parts_written = [sem(f"parts_written{b}") for b in range(B)]
        stack_loaded = [sem(f"stack_loaded{g}") for g in range(G)]
        shift_loaded = [sem(f"shift_loaded{g}") for g in range(G)]
        table_mm, table_copied = sem("table_mm"), sem("table_copied")
        bias_mm, bias_copied, bias_turned, bias_kept = (
            sem("bias_mm"), sem("bias_copied"), sem("bias_turned"), sem("bias_kept"))
        scores_ready, probs_ready, pv_done = sem("scores_ready"), sem("probs_ready"), sem("pv_done")
        sm_ready, max_ready = sem("sm_ready"), sem("max_ready")
        shift_chain, shift_split = sem("shift_chain"), sem("shift_split")
        v_ready, o_copied, rsum_ready = sem("v_ready"), sem("o_copied"), sem("rsum_ready")
        xb_ready = sem("xb_ready")
        misc_ready, misc_done, hidden_made = sem("misc_ready"), sem("misc_done"), sem("hidden_made")
        side_ready, side_done = sem("side_ready"), sem("side_done")
        dve_step, pool_step, act_step = sem("dve_step"), sem("pool_step"), sem("act_step")
        w_loaded = [sem(f"w_loaded{j}") for j in range(FJ)]
        tail_made, late_step, late_pool = sem("tail_made"), sem("late_step"), sem("late_pool")
        weighed, tail_weighed = sem("weighed"), sem("tail_weighed")
        w_written, y_made, y_stored = sem("w_written"), sem("y_made"), sem("y_stored")

        def maxima_of(u, more):
            return [(u + LEAD, c) for c in range(C) if more or u + LEAD < U]

        JOBS = {0: (["up0", "up1"], ["o3"]), 1: (["up2", "up3"], []), 2: (["shift1", "up4"], ["up5"]),
                3: (["up6"], ["up7"]), 4: ([], ["o0"]), 5: ([], ["x1t"]),
                6: (["shift2", "sim"], ["down0"]), 7: ([], ["down1"]), 8: ([], ["o1", "down2"]),
                9: (["shift3"], ["wt", "down3"]), 10: ([], ["down4"]), 11: ([], ["down5"]),
                12: ([], ["down6"]), 13: ([], ["down7"]), 14: (["shift0"], ["o2"])}
        OWN = ("shift0", "shift1", "shift2", "shift3", "o0", "o1", "o2")
        SIDE = ("o0", "x1t", "sim", "o1", "wt", f"up{FJ - 1}")

        def is_misc(n):
            return n[:2] != "up" and n not in SIDE

        def is_kept(n):
            return is_misc(n) and n[:4] != "down"

        def is_side(n):
            return n in SIDE

        FIRST, SECOND, EVERY = (True, False, True, False), (True, True, True, False), (True, True, True, True)
        LAST_ONE, TAIL = (True, True, False, True), (False, True, False, True)

        def here(n, attention, experts, more, late):
            return (late if n[:2] == "up" else attention if n in OWN else experts) and (more or n != "shift0")

        def jobs_of(kind):
            return [n for u in sorted(JOBS) for half in JOBS[u] for n in half if here(n, *kind)]

        def job(t, name, counted):
            kinds = (FIRST, SECOND, EVERY, LAST_ONE, TAIL)
            n = [len([x for x in jobs_of(kind) if counted(x)]) for kind in kinds]
            rounds_before = {0: [0] * 5, 1: [1, 0, 0, 0, 0], B - 1: [1, 1, B - 3, 0, 0], B: [1, 1, B - 3, 1, 0],
                             B + 1: [1, 1, B - 3, 1, 1]}
            prologue = 0 if counted is is_side else 1
            if isinstance(t, int):
                before = prologue + sum(a * b for a, b in zip(n, rounds_before.get(t, [1, 1, t - 2, 0, 0])))
                kind = {0: FIRST, 1: SECOND, B - 1: LAST_ONE, B: TAIL}.get(t, EVERY)
            else:
                kind = EVERY
            if isinstance(t, int) and t == B + 1:
                return before + 1
            names = jobs_of(kind)
            inside = len([x for x in names[:names.index(name)] if counted(x)]) + (1 if counted(name) else 0)
            if isinstance(t, int):
                return before + inside
            return (t - 2) * n[2] + (prologue + n[0] + n[1] + inside)

        def shift_job(t, g, counted):
            if g:
                return job(t, f"shift{g}", counted)
            return 1 if is0(t) else job(t - 1, "shift0", counted)

        TAIL_VECTOR = [j for j in range(FJ) if j % 3 != 2]
        TAIL_POOL = [j for j in range(FJ) if j % 3 == 2]

        def hidden_count(f, j):
            return f * FJ + (j + 1)

        def down_bank(t, j):
            return st_ps[:, j % 3, :] if isinstance(t, int) and t == B else mi_ps[:, :]

        def score_bank(k):
            return 1 if k == U * J - 1 else k % 3

        def scores_since(k):
            return next(n for n in range(1, 5) if score_bank((k - n) % (U * J)) == score_bank(k))

        DVE_STEPS = ["astats", "amv", "bstats", "bmv", "top", "above", "ties", "n_above", "rank", "keep", "mask",
                     "wexp", "wsum", "winv", "wscale", "w"]
        LATE_STEPS = ["cstats", "cmv"]
        POOL_STEPS = ["bias", "aeps", "acentre", "apow", "ascale", "gamma", "resid", "beps", "bcentre", "bpow",
                      "bscale", "sdiff"]
        LATE_POOL = ["ceps", "ccentre", "cpow"]
        ACT_STEPS = ["tanh0", "sexp"] + [f"tanh{j}" for j in range(1, FJ)]

        def dve_at(f, name):
            names = LATE_STEPS if name in LATE_STEPS else DVE_STEPS
            return f * len(names) + (names.index(name) + 1)

        POOL_TAIL, LATE_POOL_TAIL = ["aeps", "apow", "beps", "bpow", "sdiff"], ["ceps", "cpow"]

        def pool_at(f, name):
            tail = isinstance(f, int) and f == B - 1
            if name in LATE_POOL:
                return f * len(LATE_POOL) + ((LATE_POOL_TAIL if tail else LATE_POOL).index(name) + 1)
            return f * len(POOL_STEPS) + ((POOL_TAIL if tail else POOL_STEPS).index(name) + 1)

        def act_at(f, name):
            return f * len(ACT_STEPS) + (ACT_STEPS.index(name) + 1)

        def prep_banks(b):
            return [(st_ps[:, 0, :], st_ps[:, 1, :], st_ps[:, 2, :]), (ov_ps[:, :], mi_ps[:, :], si_ps[:, :])][b % 2]

        def bias_banks(g):
            return [(st_ps[:, 0, :], st_ps[:, 2, :]), (st_ps[:, 1, :], st_ps[:, 0, :])][(g - CG) % 2]

        def split_count(b, a):
            return 2 * (b - 1) + a + 1

        def is0(t):
            return isinstance(t, int) and t == 0

        def apart(engine):
            engine.sem_inc(waits_met, 1)

        def rounds(engine, round_):
            round_(0, *FIRST)
            round_(1, *SECOND)
            with engine.Fori(2, B - 1) as t:
                round_(t, *EVERY)
            round_(B - 1, *LAST_ONE)
            round_(B, *TAIL)

        block = ctx.enter_context(nc.Block())

        @block.sync
        def _(sp):
            def load_slice(t, g):
                if not is0(t):
                    sp.wait_ge(scores_ready, (t - 1) * (J * U) + J * C * (g + 1))
                    apart(sp)
                for a, stack in enumerate((q_stack, k_stack)):
                    src = stack_dram[t, a, g * J:(g + 1) * J]
                    sp.dma_start(stack[0:TERMS, g * J:(g + 1) * J, :], src.rearrange("h r s -> r h s")) \
                      .then_inc(stack_loaded[g], 16)

            def load_shift(t, g):
                sp.wait_ge(misc_done, shift_job(t, g, is_kept))
                sp.dma_start(q_stack[SHIFT_ROW:SHIFT_ROW + PARTS, g * J:(g + 1) * J, :]
                             .rearrange("i h (c q) -> i (h c) q", c=C), shift_rows[:, :]).then_inc(shift_loaded[g], 16)

            sp.sem_inc(y_stored, 1)
            for b in range(B):
                sp.dma_start(x_sb[:, b], x[b].rearrange("(c p) e -> p c e", p=P)).then_inc(x_loaded[b], 16)
                if b == 0:
                    for dst, src in ((wq_sb, w_q), (wk_sb, w_k), (wv_sb, w_v)):
                        sp.dma_start(dst[:], src).then_inc(proj_loaded, 16)
            sp.dma_start(beta_sb[:], bass.AP(beta.tensor, 0, [[0, P], [1, E]])).then_inc(beta_loaded, 16)
            sp.dma_start(rel_dram[0:LAST + 1, :], rel_table).then_inc(rel_written, 16)
            sp.dma_start(rel_dram[LAST + 1:, :],
                         bass.AP(rel_table.tensor, LAST * H, [[0, NWIN + P // H - LAST - 1], [1, H]])).then_inc(rel_written, 16)
            sp.wait_ge(rel_written, 32)
            sp.dma_start(rel_win[:], bass.AP(rel_dram.tensor, 0, [[H, P], [H * P, NWIN // P], [1, P]])) \
              .then_inc(rel_loaded, 16)
            sp.dma_start(hasher_sb[:], hasher_w).then_inc(keys_loaded, 16)
            sp.dma_start(keys_sb[:], keys).then_inc(keys_loaded, 16)

            def write_parts(b, heads, written):
                for a in range(2):
                    sp.wait_ge(*((first_split, 2 * a + 2) if b == 0 else (low_made, split_count(b, a))))
                    rows = stack_dram[b, a, heads].rearrange("h (d i j) s -> (h d) i j s", i=PARTS, j=PARTS)
                    for n in range(PARTS):
                        dst = rows[:, :, n, :] if a == 0 else rows[:, n, :, :]
                        sp.dma_start(dst, parts[heads.start * D:heads.stop * D, b, a]).then_inc(written, 16)

            write_parts(0, slice(0, J), first_written)
            sp.wait_ge(first_written, 2 * PARTS * 16)
            sp.wait_ge(stack_set, 2)
            load_slice(0, 0)
            write_parts(0, slice(J, H), parts_written[0])
            sp.wait_ge(parts_written[0], 2 * PARTS * 16)
            for g in range(1, G):
                load_slice(0, g)
            sp.dma_start(gamma_sb[:], bass.AP(gamma.tensor, 0, [[0, P], [1, E]])).then_inc(rows_loaded, 16)
            sp.dma_start(scale_sb[:], bass.AP(ffn_scale.tensor, 0, [[0, P], [1, 1]])).then_inc(rows_loaded, 16)
            write_parts(1, slice(0, H), parts_written[1])
            load_shift(0, 0)
            sp.dma_start(down_sb[:], values_down.rearrange("n d p -> d n p")).then_inc(experts_loaded, 16)
            sp.dma_start(up_sb[:], values_up.rearrange("(j n) p d -> (n p) j d", j=FJ)).then_inc(experts_loaded, 16)

            def round_(t, attention, experts, more, late):
                if attention:
                    if not is0(t):
                        load_slice(t, G - 1)
                    load_shift(t, 1)
                    for b in [1] if is0(t) else range(2, B) if isinstance(t, int) and t == 1 else []:
                        sp.wait_ge(parts_written[b], 2 * PARTS * 16)
                    if more:
                        load_slice(t + 1, 0)
                    load_shift(t, 2)
                    if is0(t):
                        write_parts(2, slice(0, H), parts_written[2])
                if late:
                    store(t - 2)
                if attention and more:
                    load_slice(t + 1, 1)
                if experts:
                    sp.wait_ge(side_done, job(t, "wt", is_side))
                    apart(sp)
                    sp.dma_start(w_dram.rearrange("n c q -> c n q"), w_t[:, :]).then_inc(w_written, 16)
                if attention:
                    load_shift(t, 3)
                if is0(t):
                    for b in range(3, B):
                        write_parts(b, slice(0, H), parts_written[b])
                if experts:
                    sp.wait_ge(w_written, (t - 1) * 16 + 16)
                    for j in range(FJ):
                        src = bass.AP(w_dram.tensor, j * NJ * S, [[S, NJ], [0, PD], [1, S]])
                        sp.dma_start(w_rows[:, j, :], src).then_inc(w_loaded[j], 16)
                if attention and more:
                    load_slice(t + 1, 2)
                    load_shift(t + 1, 0)

            def store(f):
                sp.wait_ge(y_made, f + 1)
                apart(sp)
                sp.dma_start(out[f].rearrange("(c p) e -> p c e", p=P), y_out[:]).then_inc(y_stored, 16)

            rounds(sp, round_)
            store(B - 1)
            sp.wait_ge(y_stored, 16 * B + 1)

        @block.gpsimd
        def _(pool):
            def split_shift(t, g):
                n, m = t * G + g, neg_max[:, g % 2, :]
                pool.wait_ge(max_ready, n * (J * C) + J * C)
                if not (is0(t) and g == 0):
                    pool.wait_ge(misc_ready, shift_job(t, g - 1, is_misc) if g else shift_job(t - 1, G - 1, is_misc))
                    apart(pool)
                nc.gpsimd.tensor_copy(shift_parts[:, 0, :], m).then_inc(shift_chain, 1)
                pool.wait_ge(shift_chain, n * 3 + 1)
                nc.gpsimd.tensor_sub(shift_res[:], m, shift_parts[:, 0, :]).then_inc(shift_chain, 1)
                pool.wait_ge(shift_chain, n * 3 + 2)
                apart(pool)
                nc.gpsimd.tensor_copy(shift_parts[:, 1, :], shift_res[:]).then_inc(shift_chain, 1)
                pool.wait_ge(shift_chain, n * 3 + 3)
                nc.gpsimd.tensor_sub(shift_parts[:, 2, :], shift_res[:], shift_parts[:, 1, :]).then_inc(shift_split, 1)

            def fetch_values(t, g):
                if not is0(t):
                    pool.wait_ge(pv_done, (t - 1) * U + C * (g + 1))
                    apart(pool)
                nc.gpsimd.tensor_copy(v_cur[:, :, g * J:(g + 1) * J, 0:D],
                                      v_all[:, :, g * J:(g + 1) * J, t, :]).then_inc(v_ready, 1)

            def norm(f, k, eps, dst, src, centre=True):
                made, done = (late_step, late_pool) if k == "c" else (dve_step, pool_step)
                m, v, scale = (late_mv, late_veps, late_rstd) if k == "c" else (mv, veps, rstd)
                pool.wait_ge(made, dve_at(f, k + "mv"))
                apart(pool)
                nc.gpsimd.tensor_scalar(v[:], m[:, :, 1], eps, None, ALU.add).then_inc(done, 1)
                if centre:
                    nc.gpsimd.tensor_tensor(dst, src, m[:, :, 0:1].to_broadcast([P, C, E]), ALU.subtract) \
                        .then_inc(done, 1)
                pool.wait_ge(done, pool_at(f, k + "eps"))
                nc.gpsimd.tensor_tensor(scale[:], v[:], minus_half[:], ALU.pow).then_inc(done, 1)
                if centre:
                    pool.wait_ge(done, pool_at(f, k + "pow"))
                    return nc.gpsimd.tensor_tensor(dst, dst, scale[:].unsqueeze(2).to_broadcast([P, C, E]), ALU.mult)

            def weigh(f, t, j):
                pool.wait_ge(hidden_made, hidden_count(f, j))
                pool.wait_ge(w_loaded[j], f * 16 + 16)
                nc.gpsimd.tensor_tensor(hid[:, j], hid[:, j], w_rows[:, j], ALU.mult).then_inc(weighed, 1)

            def low_parts(b):
                for a in range(2):
                    pool.wait_ge(mid_made, split_count(b, a))
                    nc.gpsimd.tensor_sub(parts[:, b, a, 2, :], resid[:, b % 2, a], parts[:, b, a, 1, :]) \
                        .then_inc(low_made, 1)

            nc.gpsimd.memset(ident[:], 0.0).then_inc(consts_made, 1)
            pool.wait_ge(consts_made, 1)
            nc.gpsimd.affine_select(out=ident[:], in_=ident[:], compare_op=ALU.not_equal, fill=1.0, base=0,
                                    pattern=[[-1, P]], channel_multiplier=1).then_inc(consts_made, 1)
            two_ones = 1.0019378662109375
            pool.wait_ge(consts_made, 2)
            nc.gpsimd.memset(k_stack[64:P].bitcast(F32), two_ones).then_inc(stack_set, 1)
            pool.wait_ge(stack_set, 1)
            nc.gpsimd.memset(q_stack[64:P].bitcast(F32), 0.0).then_inc(stack_set, 1)
            pool.wait_ge(stack_set, 2)
            nc.gpsimd.memset(v_cur[:], 0.0).then_inc(consts_made, 1)
            nc.gpsimd.memset(minus_half[:], -0.5).then_inc(consts_made, 1)
            nc.gpsimd.memset(zeros[:], 0.0).then_inc(consts_made, 1)
            nc.gpsimd.memset(shift_parts[:], 0.0).then_inc(consts_made, 1)
            pool.wait_ge(consts_made, 6)
            nc.gpsimd.tensor_copy(ident_bf[:], ident[:]).then_inc(consts_made, 1)
            nc.gpsimd.memset(v_cur[:, :, :, D:D + 1], 1.0).then_inc(consts_made, 1)
            pool.wait_ge(consts_made, 8)
            pool.wait_ge(beta_loaded, 16)
            for b in range(B):
                pool.wait_ge(prep_mm, 4 * b + 1)
                nc.gpsimd.tensor_tensor(x_sb[:, b], x_sb[:, b], beta_sb[:].unsqueeze(1).to_broadcast([P, C, E]),
                                        ALU.add).then_inc(xb_ready, 1)
                if b >= 2:
                    low_parts(b - 1)
            for g in range(G):
                fetch_values(0, g)
            low_parts(B - 1)
            split_shift(0, 0)

            def round_(t, attention, experts, more, late):
                f = t - 1
                if attention and not is0(t):
                    fetch_values(t, G - 1)
                if experts and attention:
                    pool.wait_ge(misc_done, job(t, "o3", is_kept))
                    nc.gpsimd.tensor_tensor(z[:].rearrange("p c (h d) -> p c h d", d=D),
                                            attn[:].rearrange("p c (h d) -> p c h d", d=D),
                                            bias_v[:, :, :, f, :], ALU.add).then_inc(pool_step, 1)
                if attention:
                    split_shift(t, 1)
                if experts and not attention:
                    norm(f, "a", EPS_ATTENTION, None, None, centre=False)
                    norm(f, "b", EPS_LN, None, None, centre=False)
                    late_norm(t - 2)
                elif experts:
                    norm(f, "a", EPS_ATTENTION, z[:], z[:]).then_inc(pool_step, 1)
                    pool.wait_ge(pool_step, pool_at(f, "ascale"))
                    nc.gpsimd.tensor_tensor(z[:], z[:], gamma_sb[:].unsqueeze(1).to_broadcast([P, C, E]),
                                            ALU.mult).then_inc(pool_step, 1)
                    pool.wait_ge(pool_step, pool_at(f, "gamma"))
                    nc.gpsimd.tensor_tensor(z[:], z[:], x_sb[:, f], ALU.add).then_inc(pool_step, 1)
                    if late:
                        pool.wait_ge(side_done, job(t, f"up{FJ - 1}", is_side))
                    norm(f, "b", EPS_LN, x1[:], z[:]).then_inc(pool_step, 1)
                if attention:
                    split_shift(t, 2)
                    if late:
                        late_norm(t - 2)
                    if more:
                        fetch_values(t + 1, 0)
                if experts:
                    pool.wait_ge(dve_step, dve_at(f, "top"))
                    nc.gpsimd.tensor_tensor(sdiff[:], sim[:], top[:, :, 0:1].to_broadcast([P, C, NE]),
                                            ALU.subtract).then_inc(pool_step, 1)
                if attention:
                    if more:
                        fetch_values(t + 1, 1)
                    split_shift(t, 3)
                if experts:
                    for j in range(FJ // 2) if attention else TAIL_POOL:
                        weigh(f, t, j)
                if attention:
                    if more:
                        fetch_values(t + 1, 2)
                    if experts:
                        for j in range(FJ // 2, FJ - 2):
                            weigh(f, t, j)
                    if more:
                        split_shift(t + 1, 0)
                    if experts:
                        for j in range(FJ - 2, FJ):
                            weigh(f, t, j)

            def late_norm(f):
                pool.wait_ge(y_stored, f * 16 + 1)
                norm(f, "c", EPS_LN, y_out[:], y[:]).then_inc(y_made, 1)

            rounds(pool, round_)
            norm(B - 1, "c", EPS_LN, None, None, centre=False)

        @block.scalar
        def _(act):
            def copy(dst, src, scale=1.0):
                return nc.scalar.activation(dst, src, ACT.Copy, scale=scale)

            def middle_parts(b):
                for a in range(2):
                    act.wait_ge(resid_made, 2 * b + a + 1)
                    copy(parts[:, b, a, 1, :], resid[:, b % 2, a]).then_inc(mid_made, 1)

            for b in range(B):
                turned, q_made, k_made = prep_banks(b)
                act.wait_ge(prep_mm, 4 * b + 1)
                copy(x_t[:, b % 2, :], turned).then_inc(prep_copied, 1)
                if b >= 2:
                    middle_parts(b - 1)
                for a, made in enumerate((q_made, k_made)):
                    act.wait_ge(prep_mm, 4 * b + 2 + a)
                    copy(parts[:, b, a, 0, :], made).then_inc(prep_copied, 1)
                act.wait_ge(prep_mm, 4 * b + 4)
                copy(v_all[:, :, :, b, :].rearrange("p c h d -> p (c h) d"),
                     turned.rearrange("p (n d) -> p n d", d=D)).then_inc(prep_copied, 1)
            act.wait_ge(table_mm, 1)
            copy(rel_t[:], st_ps[:, 0, :]).then_inc(table_copied, 1)
            act.wait_ge(table_mm, 2)
            copy(keys_t[:], st_ps[0:PD, 1, 0:NE]).then_inc(table_copied, 1)
            act.wait_ge(table_mm, 3)
            copy(sim_w[:], st_ps[:, 2, 0:NE]).then_inc(table_copied, 1)

            middle_parts(B - 1)

            def bias_copy(g):
                act.wait_ge(bias_mm, g - CG + 2)
                if g >= CG + 2:
                    act.wait_ge(bias_turned, g - CG - 1)
                n = constant_from((g + 1) * J - 1) + 1
                turned = bias_t[:, g % 2, :].rearrange("p (a r) -> p r a", r=H)
                made = bias_banks(g)[0][:, 0:n * HPB].rearrange("p (r a) -> p r a", r=n)
                copy(turned[:, 0:n, :], made)
                copy(turned[:, n:, :], made[:, n - 1:n, :].to_broadcast([P, H - n, HPB])).then_inc(bias_copied, 1)

            def bias_keep(g):
                act.wait_ge(bias_turned, g - CG + 1)
                copy(bias_v[:, :, g * J:(g + 1) * J].rearrange("p c j b d -> p c (j b d)"),
                     bias_banks(g)[1].rearrange("p (c n) -> p c n", c=C)).then_inc(bias_kept, 1)

            def bias_spread():
                act.wait_ge(bias_mm, 1)
                n = CG * J * B * D
                copy(bias_v[:, :, 0:CG * J].rearrange("p c h b d -> p c (h b d)"),
                     st_ps[:, 2, 0:n].unsqueeze(1).to_broadcast([P, C, n])).then_inc(bias_kept, 1)

            def shift_copy(t, g):
                act.wait_ge(misc_ready, shift_job(t, g, is_misc))
                if not (is0(t) and g == 0):
                    act.wait_ge(shift_loaded[(g - 1) % G], 16 * (t if g == 0 else t + 1))
                copy(shift_rows[:, :], mi_bf[0:PARTS * J * C, 0:P]).then_inc(misc_done, 1)

            mi_bf = mi_ps[:, :].bitcast(BF16)
            bias_spread()
            for g in range(CG, G):
                bias_copy(g)
                if g == CG:
                    shift_copy(0, 0)
                if g > CG:
                    bias_keep(g - 1)
            bias_keep(G - 1)
            act.wait_ge(rows_loaded, 32)
            copy(half_scale[:], scale_sb[:], 0.5).then_inc(table_copied, 1)

            def exp(t, u, j):
                n = t * U + u
                act.wait_ge(scores_ready, J * n + j + 1)
                if j == 0 and not (is0(t) and u < 2):
                    act.wait_ge(pv_done, n - 1)
                nc.scalar.activation(probs[:, u % 2, j, :], st_ps[:, score_bank(u * J + j), :], ACT.Exp,
                                     scale=SCORE_SCALE).then_inc(probs_ready, 1)

            def o_copy(t, g, in_round):
                act.wait_ge(pv_done, t * U + C * (g + 1))
                if not (is0(t) and g == 0):
                    name = f"o{(g - 1) % G}"
                    act.wait_ge(*((side_ready, job(in_round, name, is_side)) if is_side(name) else
                                  (misc_ready, job(in_round, name, is_misc))))
                copy(o_sb[:], ov_ps[:]).then_inc(o_copied, 1)

            def expert_copy(t, name):
                f = t - 1
                if name == "x1t":
                    act.wait_ge(side_ready, job(t, name, is_side))
                    copy(x1_t[:], si_ps[:]).then_inc(side_done, 1)
                    return
                if name == "sim":
                    act.wait_ge(side_ready, job(t, name, is_side))
                    copy(sim[:].rearrange("p c n -> p (c n)"), si_ps[:, 0:C * NE]).then_inc(side_done, 1)
                    return
                if name == "wt":
                    act.wait_ge(side_ready, job(t, name, is_side))
                    copy(w_t[:], si_ps[:, 0:P]).then_inc(side_done, 1)
                else:
                    act.wait_ge(misc_ready, job(t, name, is_misc))
                    j = int(name[4:])
                    nc.scalar.activation(tanh_sb[:, j % 3, :], down_bank(t, j), ACT.Tanh, scale=0.5).then_inc(act_step, 1)

            def round_(t, attention, experts, more, late):
                def copies(half):
                    for name in half:
                        if name.startswith("shift") and here(name, attention, experts, more, late):
                            shift_copy(*((t, int(name[5:])) if name != "shift0" else (t + 1, 0)))
                        elif name in ("x1t", "sim", "wt") or name.startswith("down"):
                            if experts:
                                expert_copy(t, name)

                for u in range(U):
                    before, behind = JOBS.get(u, ([], []))
                    if attention:
                        for j in range(J - 1):
                            exp(t, u, j)
                    if u == 0 and experts:
                        o_copy(t - 1, G - 1, t - 1)
                    if u and u % C == 0 and attention:
                        o_copy(t, u // C - 1, t)
                    copies(before)
                    if u == 7 and experts:
                        act.wait_ge(pool_step, pool_at(t - 1, "sdiff"))
                        nc.scalar.activation(sexp[:], sdiff[:], ACT.Exp).then_inc(act_step, 1)
                    if attention:
                        exp(t, u, J - 1)
                    copies(behind)

            rounds(act, round_)

        @block.vector
        def _(dve):
            def resids(b):
                for a in range(2):
                    dve.wait_ge(prep_copied, 4 * b + 2 + a)
                    if b >= 2:
                        dve.wait_ge(*((first_split, 2 * a + 2) if b == 2 else (low_made, split_count(b - 2, a))))
                    nc.vector.tensor_sub(resid[:, b % 2, a], prep_banks(b)[1 + a], parts[:, b, a, 0, :]) \
                        .then_inc(resid_made, 1)
                    if b == 0:
                        dve.wait_ge(resid_made, a + 1)
                        nc.vector.tensor_copy(parts[:, b, a, 1, :], resid[:, 0, a]).then_inc(first_split, 1)
                        dve.wait_ge(first_split, 2 * a + 1)
                        nc.vector.tensor_sub(parts[:, b, a, 2, :], resid[:, 0, a], parts[:, b, a, 1, :]) \
                            .then_inc(first_split, 1)

            for b in range(B - 1):
                resids(b)

            def maximum(t, pos, c):
                n, g = t * U + pos, (pos // J) % G
                dve.wait_ge(sm_ready, C * n + c + 1)
                if pos % J == 0 and c == 0 and not (is0(t) and pos // J < 2):
                    dve.wait_ge(shift_split, t * G + pos // J - 1)
                col = (pos % J) * C + c
                nc.vector.tensor_reduce(neg_max[:, g % 2, col:col + 1], sm_ps[:, c % 2, :], AX.X, ALU.max,
                                        negate=True).then_inc(max_ready, 1)

            BEFORE_RESIDS = 6
            for k in range(EARLY):
                if k == BEFORE_RESIDS:
                    resids(B - 1)
                maximum(0, *divmod(k, C))

            def attend(t, g, in_round):
                name = f"o{g}"
                if is_side(name):
                    dve.wait_ge(side_ready, job(in_round, name, is_side))
                else:
                    dve.wait_ge(misc_ready, job(in_round, name, is_misc))
                bank, done = (si_ps, side_done) if is_side(name) else (mi_ps, misc_done)
                o = bank[:].rearrange("p (c j w) -> p c j w", c=C, j=J)
                n = t * G + g
                nc.vector.reciprocal(rsum[:], o[:, :, :, D]).then_inc(rsum_ready, 1)
                dve.wait_ge(rsum_ready, n + 1)
                nc.vector.tensor_tensor(attn[:, :, g * J * D:(g + 1) * J * D].rearrange("p c (j d) -> p c j d", d=D),
                                        o[:, :, :, 0:D], rsum[:].unsqueeze(3).to_broadcast([P, C, J, D]),
                                        ALU.mult).then_inc(done, 1)

            def norm_buffers(k):
                return (late_stats, late_mv, late_step) if k == "c" else (stats, mv, dve_step)

            def stats_of(f, k, src):
                into, _, done = norm_buffers(k)
                for c in range(C):
                    i = nc.vector.bn_stats(into[:, c, :], src[:, c, :])
                i.then_inc(done, 1)

            def mv_of(f, k):
                of, into, done = norm_buffers(k)
                dve.wait_ge(done, dve_at(f, k + "stats"))
                apart(dve)
                for c in range(C):
                    i = nc.vector.bn_aggr(into[:, c, :], of[:, c, :])
                i.then_inc(done, 1)

            def after(f, name):
                dve.wait_ge(dve_step, dve_at(f, name))

            def step(i):
                i.then_inc(dve_step, 1)

            def flat(a):
                return a[:].rearrange("p c n -> p (c n)")

            def hidden(t, j):
                dve.wait_ge(act_step, act_at(t - 1, f"tanh{j}"))
                nc.vector.scalar_tensor_tensor(out=hid[:, j], in0=tanh_sb[:, j % 3, :], scalar=1.0, in1=down_bank(t, j),
                                               op0=ALU.add, op1=ALU.mult).then_inc(hidden_made, 1)

            def tail_norms(f):
                def normed(k, dst, n):
                    dve.wait_ge(pool_step, pool_at(f, k + "pow"))
                    for c in range(C):
                        i = nc.vector.tensor_scalar(dst[:, c, :], z[:, c, :], mv[:, c, 0:1], rstd[:, c:c + 1],
                                                    ALU.subtract, ALU.mult)
                    i.then_inc(tail_made, 1)
                    dve.wait_ge(tail_made, n)

                dve.wait_ge(misc_done, job(f + 1, "o3", is_kept))
                nc.vector.tensor_tensor(z[:].rearrange("p c (h d) -> p c h d", d=D),
                                        attn[:].rearrange("p c (h d) -> p c h d", d=D),
                                        bias_v[:, :, :, f, :], ALU.add).then_inc(tail_made, 1)
                dve.wait_ge(tail_made, 1)
                stats_of(f, "a", z)
                mv_of(f, "a")
                normed("a", z, 2)
                nc.vector.tensor_tensor(z[:], z[:], gamma_sb[:].unsqueeze(1).to_broadcast([P, C, E]),
                                        ALU.mult).then_inc(tail_made, 1)
                dve.wait_ge(tail_made, 3)
                nc.vector.tensor_tensor(z[:], z[:], x_sb[:, f], ALU.add).then_inc(tail_made, 1)
                dve.wait_ge(tail_made, 4)
                stats_of(f, "b", z)
                mv_of(f, "b")
                late_y(f - 1, B)
                late_stats_of(f - 1, B)
                normed("b", x1, 5)
                mv_of(f - 1, "c")

            def expert_steps(t, u, s, attention, late):
                f = t - 1
                at = (u, s)
                if at == (1, 0):
                    attend(f, G - 1, t)
                    if not attention:
                        tail_norms(f)
                elif at < (5, 0) and not attention:
                    return
                elif at == (1, 3):
                    dve.wait_ge(pool_step, pool_at(f, "bias"))
                    stats_of(f, "a", z)
                elif at == (2, 0):
                    mv_of(f, "a")
                elif at == ((3, 2) if late else (4, 1)):
                    dve.wait_ge(pool_step, pool_at(f, "resid"))
                    stats_of(f, "b", z)
                elif at == ((3, 3) if late else (4, 2)):
                    mv_of(f, "b")
                elif at == (6, 3):
                    dve.wait_ge(side_done, job(t, "sim", is_side))
                    apart(dve)
                    for c in range(C):
                        i = nc.vector.max(top[:, c, :], sim[:, c, :])
                    step(i)
                elif at == (7, 1):
                    after(f, "top")
                    fourth = top[:, :, TOPK - 1:TOPK].to_broadcast([P, C, NE])
                    step(nc.vector.tensor_tensor(above[:], sim[:], fourth, ALU.is_gt))
                    step(nc.vector.tensor_tensor(ties[:], sim[:], fourth, ALU.is_equal))
                elif at == (7, 2):
                    after(f, "above")
                    step(nc.vector.tensor_reduce(n_above[:], above[:], AX.X, ALU.add))
                elif at == (7, 3):
                    after(f, "n_above")
                    for c in range(C):
                        i = nc.vector.tensor_tensor_scan(rank[:, c, :], ties[:, c, :], zeros[:], n_above[:, c:c + 1],
                                                         ALU.add, ALU.add)
                    step(i)
                elif at == (8, 1):
                    after(f, "rank")
                    step(nc.vector.scalar_tensor_tensor(out=flat(keep), in0=flat(rank), scalar=float(TOPK),
                                                        in1=flat(ties), op0=ALU.is_le, op1=ALU.mult))
                elif at == (8, 2):
                    after(f, "keep")
                    step(nc.vector.tensor_tensor(mask[:], keep[:], above[:], ALU.add))
                    after(f, "mask")
                    dve.wait_ge(act_step, act_at(f, "sexp"))
                    step(nc.vector.tensor_tensor(wexp[:], sexp[:], mask[:], ALU.mult))
                elif at == (8, 3):
                    after(f, "wexp")
                    step(nc.vector.tensor_reduce(wsum[:], wexp[:], AX.X, ALU.add))
                    after(f, "wsum")
                    step(nc.vector.reciprocal(winv[:], wsum[:]))
                elif at == (9, 1):
                    after(f, "winv")
                    step(nc.vector.tensor_scalar(wscale[:], winv[:], half_scale[:, 0:1], None, ALU.mult))
                    after(f, "wscale")
                    step(nc.vector.tensor_tensor(w_tok[:], wexp[:], wscale[:].unsqueeze(2).to_broadcast([P, C, NE]),
                                                 ALU.mult))
                    if not attention:
                        for j in range(3):
                            hidden(t, j)
                if s == 0 and 7 <= u < 7 + FJ and (attention or u >= 10):
                    hidden(t, u - 7)

            def late_y(f, in_round):
                dve.wait_ge(side_ready, job(in_round, f"up{FJ - 1}", is_side))
                nc.vector.scalar_tensor_tensor(out=flat(y), in0=flat(x1), scalar=2.0, in1=si_ps[:],
                                               op0=ALU.mult, op1=ALU.add).then_inc(side_done, 1)

            def late_stats_of(f, in_round):
                dve.wait_ge(side_done, job(in_round, f"up{FJ - 1}", is_side))
                stats_of(f, "c", y)

            def round_(t, attention, experts, more, late):
                for u in range(U):
                    maxima = maxima_of(u, more) if attention else []
                    for s in range(C):
                        if s < len(maxima):
                            maximum(t, *maxima[s])
                        if attention and s == 0 and u in (5, 9, 15):
                            g = {5: 0, 9: 1, 15: 2}[u]
                            attend(t, g, t)
                        if late and attention:
                            if (u, s) == (4, 0):
                                late_y(t - 2, t)
                            elif (u, s) == (4, 2):
                                late_stats_of(t - 2, t)
                            elif (u, s) == (4, 3):
                                mv_of(t - 2, "c")
                        if experts:
                            expert_steps(t, u, s, attention, late)

            rounds(dve, round_)
            f = B - 1
            for j in TAIL_VECTOR:
                dve.wait_ge(hidden_made, hidden_count(f, j))
                dve.wait_ge(w_loaded[j], f * 16 + 16)
                nc.vector.tensor_tensor(hid[:, j], hid[:, j], w_rows[:, j], ALU.mult).then_inc(tail_weighed, 1)
            dve.wait_ge(y_made, B - 1)
            late_y(f, B + 1)
            late_stats_of(f, B + 1)
            mv_of(f, "c")
            dve.wait_ge(late_pool, pool_at(f, "cpow"))
            dve.wait_ge(y_stored, f * 16 + 1)
            for c in range(C):
                i = nc.vector.tensor_scalar(y_out[:, c, :], y[:, c, :], late_mv[:, c, 0:1], late_rstd[:, c:c + 1],
                                            ALU.subtract, ALU.mult)
            i.then_inc(y_made, 1)

        @block.tensor
        def _(pe):
            mi_bf = mi_ps[:, :].bitcast(BF16)
            pitch = rel_t[:, :].ap[0][0]

            def prep(b):
                if b == 0:
                    pe.wait_ge(consts_made, 2)
                pe.wait_ge(x_loaded[b], 16)
                if b >= 2:
                    pe.wait_ge(prep_copied, 4 * (b - 2) + 4)
                    pe.wait_ge(resid_made, 2 * (b - 2) + 2)
                turned, q_made, k_made = prep_banks(b)
                for c in range(C):
                    i = nc.tensor.transpose(turned[:, c * P:(c + 1) * P], x_sb[:, b, c, :], ident[:])
                i.then_inc(prep_mm, 1)
                if b == B - 1:
                    early_maxima(1)
                if b == 0:
                    pe.wait_ge(proj_loaded, 48)
                pe.wait_ge(prep_copied, 4 * b + 1)
                xt = x_t[:, b % 2, :]
                nc.tensor.matmul(q_made, wq_sb[:], xt, start=True, stop=True).then_inc(prep_mm, 1)
                nc.tensor.matmul(k_made, wk_sb[:], xt, start=True, stop=True).then_inc(prep_mm, 1)
                if b == B - 1:
                    early_maxima(1)
                for c in range(C):
                    i = nc.tensor.matmul(turned[:, c * P:(c + 1) * P], xt[:, c * P:(c + 1) * P],
                                         wv_sb[:], start=True, stop=True)
                i.then_inc(prep_mm, 1)

            def maximum_scores(t, pos, c):
                n, h = t * U + pos, pos % U
                k = C * n + c
                if pos % J == 0 and c == 0:
                    pe.wait_ge(stack_loaded[pos // J % G], 32 * (t + pos // U) + 32)
                if not (is0(t) and pos == 0 and c < 2):
                    pe.wait_ge(max_ready, k - 1)
                nc.tensor.matmul(sm_ps[:, c % 2, :], q_stack[0:SHIFT_ROW, h, c * P:(c + 1) * P],
                                 k_stack[0:SHIFT_ROW, h, :], start=True, stop=True).then_inc(sm_ready, 1)

            def scores(t, u, j):
                n, g, kc, k = t * U + u, u // C, u % C, u * J + j
                if j == 0 and kc == 0:
                    pe.wait_ge(shift_loaded[g], 16 * t + 16)
                if not (is0(t) and k < 3):
                    pe.wait_ge(probs_ready, J * n + j + 1 - scores_since(k))
                nc.tensor.matmul(st_ps[:, score_bank(k), :], k_stack[:, g * J + j, kc * P:(kc + 1) * P],
                                 q_stack[:, g * J + j, :], start=True, stop=True).then_inc(scores_ready, 1)

            def values(t, u):
                n, g, kc = t * U + u, u // C, u % C
                if kc == 0:
                    pe.wait_ge(v_ready, t * G + g + 1)
                    if not (is0(t) and g == 0):
                        pe.wait_ge(o_copied, t * G + g)
                pe.wait_ge(probs_ready, J * n + J)
                for j in range(J):
                    i = nc.tensor.matmul(ov_ps[j * TILE:(j + 1) * TILE, :], v_cur[:, kc, g * J + j, :],
                                         probs[:, u % 2, j, :], start=(kc == 0), stop=(kc == C - 1))
                i.then_inc(pv_done, 1)

            def turn(dst, src, idn):
                return nc.tensor.transpose(dst, src, idn)

            def up(f, j, in_round):
                if j == 0:
                    count = job(in_round, f"up{FJ - 1}", is_side) - 1
                    if not isinstance(in_round, int) or count > 0:
                        pe.wait_ge(side_done, count)
                if isinstance(f, int) and f == B - 1:
                    pe.wait_ge(*((tail_weighed, TAIL_VECTOR.index(j) + 1) if j in TAIL_VECTOR else
                                 (weighed, f * FJ + TAIL_POOL.index(j) + 1)))
                else:
                    pe.wait_ge(weighed, hidden_count(f, j))
                for c in range(C):
                    i = nc.tensor.matmul(si_ps[:, c * P:(c + 1) * P], hid[:, j, c * P:(c + 1) * P], up_sb[:, j, :],
                                         start=(j == 0 and c == 0), stop=(j == FJ - 1), skip_group_check=True)
                if j == FJ - 1:
                    i.then_inc(side_ready, 1)

            def misc(t, name, kind):
                f = t - 1
                if name.startswith("up"):
                    up(t - 2, int(name[2:]), t)
                    return
                bank, ready = (si_ps, side_ready) if is_side(name) else (mi_ps, misc_ready)
                if is_side(name):
                    count = job(t, name, is_side) - 1
                    if not isinstance(t, int) or count > 0:
                        pe.wait_ge(side_done, count)
                elif not (name.startswith("down") and down_bank(t, 0) is not mi_ps and isinstance(t, int) and t == B):
                    count = job(t, name, is_kept)
                    pe.wait_ge(misc_done, count - 1 if is_kept(name) else count)
                    names = [n for n in jobs_of(kind) if is_misc(n)]
                    last = names[names.index(name) - 1] if names[0] != name else name
                    if last != name and last.startswith("down"):
                        pe.wait_ge(hidden_made, hidden_count(f, int(last[4:])))
                elif int(name[4:]) >= 3:
                    pe.wait_ge(hidden_made, hidden_count(f, int(name[4:]) - 3))
                if name.startswith("o"):
                    g = int(name[1:])
                    pe.wait_ge(o_copied, (f if g == G - 1 else t) * G + g + 1)
                    for c in range(C):
                        i = turn(bank[:, c * P:(c + 1) * P], o_sb[:, c * P:(c + 1) * P], ident[:])
                elif name.startswith("shift"):
                    g = int(name[5:])
                    pe.wait_ge(shift_split, (t + 1 if g == 0 else t) * G + g + 1)
                    i = turn(mi_bf[:, 0:P], shift_parts[:].rearrange("p i n -> p (i n)"), ident_bf[:])
                elif name == "x1t":
                    if kind[0]:
                        pe.wait_ge(pool_step, pool_at(f, "bscale"))
                    else:
                        pe.wait_ge(tail_made, 5)
                    for c in range(C):
                        i = turn(bank[:, c * P:(c + 1) * P], x1[:, c, :], ident[:])
                elif name == "sim":
                    pe.wait_ge(side_done, job(t, "x1t", is_side))
                    for c in range(C):
                        i = nc.tensor.matmul(bank[:, c * NE:(c + 1) * NE], x1_t[:, c * P:(c + 1) * P], sim_w[:],
                                             start=True, stop=True)
                elif name == "wt":
                    pe.wait_ge(dve_step, dve_at(f, "w"))
                    i = turn(bank[:, 0:P], w_tok[:].rearrange("p c n -> p (c n)"), ident[:])
                else:
                    j = int(name[4:])
                    if j == 0:
                        pe.wait_ge(experts_loaded, 32)
                    i = nc.tensor.matmul(down_bank(t, j), down_sb[:, j * NJ:(j + 1) * NJ, :], x1_t[:],
                                         start=True, stop=True)
                i.then_inc(ready, 1)

            early = [divmod(k, C) for k in range(EARLY)]

            def early_maxima(n, most=J * C + 2):
                for _ in range(n):
                    if early and EARLY - len(early) < most:
                        maximum_scores(0, *early.pop(0))

            for b in range(B - 1):
                prep(b)
            early_maxima(2)
            prep(B - 1)
            early_maxima(2)
            pe.wait_ge(rel_loaded, 16)
            pe.wait_ge(prep_copied, 4 * (B - 1) + 4)
            pe.wait_ge(resid_made, 2 * (B - 2) + 2)
            for n in range(NWIN // P):
                i = turn(st_ps[:, 0, n * P:(n + 1) * P], rel_win[:, n, :], ident[:])
            i.then_inc(table_mm, 1)
            pe.wait_ge(keys_loaded, 32)
            early_maxima(1)
            turn(st_ps[0:PD, 1, 0:NE], keys_sb[:], ident[0:NE, 0:NE]).then_inc(table_mm, 1)
            early_maxima(1)
            pe.wait_ge(table_copied, 2)
            nc.tensor.matmul(st_ps[:, 2, 0:NE], hasher_sb[:], keys_t[:], start=True, stop=True).then_inc(table_mm, 1)

            pe.wait_ge(table_copied, 3)
            for kc in range(C):
                i = nc.tensor.matmul(st_ps[:, 2, 0:CG * J * B * D], rel_t[:, LAST:LAST + P],
                                     v_all[:, kc, 0:CG * J].rearrange("p h b d -> p (h b d)"),
                                     start=(kc == 0), stop=(kc == C - 1))
                early_maxima(1 + kc % 2)
            i.then_inc(bias_mm, 1)

            def bias_turn(g):
                pe.wait_ge(bias_copied, g - CG + 1)
                pe.wait_ge(bias_kept, g - CG + 1) if g == CG else pe.wait_ge(bias_copied, 2)
                for c in range(C):
                    i = turn(bias_banks(g)[1][:, c * P:(c + 1) * P], bias_t[:, g % 2, c * P:(c + 1) * P], ident[:])
                i.then_inc(bias_turned, 1)

            for g in range(CG, G):
                if g >= CG + 2:
                    pe.wait_ge(bias_copied, g - CG - 1)
                n = constant_from((g + 1) * J - 1) + 1
                for kc in range(C):
                    for j in range(J):
                        h = g * J + j
                        window = bass.AP(rel_t, S - 1 - HPB * h + (P // H) * kc, [[pitch, P], [HPB, n], [-1, HPB]])
                        i = nc.tensor.matmul(bias_banks(g)[0][j * TILE:(j + 1) * TILE, 0:n * HPB],
                                             v_all[:, kc, h].rearrange("p b d -> p (b d)"), window, start=(kc == 0), stop=(kc == C - 1))
                    if kc == C - 1:
                        i.then_inc(bias_mm, 1)
                    early_maxima(1, J * C + 2 if g == CG else EARLY)
                if g == CG:
                    early_maxima(EARLY)
                    pe.wait_ge(resid_made, 2 * B)
                    pe.wait_ge(consts_made, 8)
                    pe.wait_ge(shift_split, 1)
                    turn(mi_bf[:, 0:P], shift_parts[:].rearrange("p i n -> p (i n)"), ident_bf[:]) \
                        .then_inc(misc_ready, 1)
                if g > CG:
                    bias_turn(g - 1)
                    early_maxima(2, EARLY)
            bias_turn(G - 1)
            early_maxima(EARLY, EARLY)
            pe.wait_ge(bias_kept, G - CG + 1)

            def round_(t, attention, experts, more, late):
                kind = (attention, experts, more, late)

                def jobs(half):
                    for name in half:
                        if here(name, *kind):
                            misc(t, name, kind)

                for u in range(U):
                    before, behind = JOBS.get(u, ([], []))

                    if not attention and u == 0:
                        before, behind = behind, before
                    todo = maxima_of(u, more) if attention else []

                    def maxima(k):
                        for pos_c in todo[k:k + 1]:
                            maximum_scores(t, *pos_c)

                    def score(*heads):
                        for j in heads:
                            if attention:
                                scores(t, u, j)
                    spread = not any(here(n, *kind) and n[:2] in ("do", "up") for n in JOBS.get(u - 1, ([], []))[1])
                    score(*range(1 + spread))
                    maxima(0)
                    score(*range(1 + spread, 3))
                    maxima(1)
                    if u and attention:
                        values(t, u - 1)
                    elif u == 0 and experts:
                        values(t - 1, U - 1)
                    maxima(2)
                    jobs(before)
                    score(3)
                    maxima(3)
                    jobs(behind)

            rounds(pe, round_)
            for j in range(FJ):
                up(B - 1, j, B + 1)


_INS = ["L0_attn_x", "L0_attn_Wq", "L0_attn_Wk", "L0_attn_Wv", "L0_attn_rel_table", "L0_attn_gamma", "L0_attn_beta",
        "L0_ffn_hasher_w", "L0_ffn_keys", "L0_ffn_values_down", "L0_ffn_values_up", "L0_ffn_scale"]


def kernel(**inputs):
    import numpy as np
    import concourse.bacc as bacc
    from concourse import mybir as _mybir
    from concourse.bass_utils import run_bass_kernel_spmd

    nc = bacc.Bacc("TRN2", target_bir_lowering=False, num_devices=1)
    arrays, args = {}, []
    for name in _INS:
        a = np.ascontiguousarray(inputs[name])
        arrays[name] = a
        args.append(nc.dram_tensor(name, a.shape, _mybir.dt.from_np(a.dtype), kind="ExternalInput").ap())
    shape = arrays["L0_attn_x"].shape
    args.append(nc.dram_tensor("out", shape, _mybir.dt.float32, kind="ExternalOutput").ap())
    bass_postln_attention_product_key_ffn(nc, *args)
    return run_bass_kernel_spmd(nc, [arrays], core_ids=[0]).results[0]["out"]
```
